# Optimizing a Trainium2 kernel written in Bass

```python
import numpy as np
import jax
import jax.numpy as jnp

def _softmax(x, axis=-1):
    return jax.nn.softmax(x, axis=axis)

def _gelu(x):
    return jax.nn.gelu(x, approximate=True)

def _silu(x):
    return jax.nn.silu(x)

def _sigmoid(x):
    return jax.nn.sigmoid(x)

def _layernorm(x, axis=-1, eps=1e-05):
    m = jnp.mean(x, axis=axis, keepdims=True)
    v = jnp.var(x, axis=axis, keepdims=True)
    return (x - m) / jnp.sqrt(v + eps)

def _scatter_add(tgt, idx, src, axis=0):
    return tgt.at[idx].add(src)

def _segment_sum(src, seg, n):
    return jax.ops.segment_sum(src, seg, n)
kernel_name = 'mk_gnn_preln_d1_gnn_r64_00b106'

def setup_inputs(seed: int=0):
    np.random.seed(seed)
    _w = jnp.asarray

    def _rec_inputs():
        import jax
        import jax.numpy as jnp
        _gk = jax.random.key(seed)
        x = -0.0003713 + 1 * jax.random.normal(jax.random.fold_in(_gk, 1), (100000, 128), jnp.float32)
        src = jax.random.randint(jax.random.fold_in(_gk, 2), (25000,), 0, 100000, jnp.int32)
        dst = jnp.minimum((100000 * jax.random.uniform(jax.random.fold_in(_gk, 3), (25000,)) ** 2.0).astype(jnp.int32), 99999)
        _o = jnp.argsort(dst, stable=True)
        src = src[_o]
        dst = dst[_o]
        return (x, src, dst)
    x, src, dst = _rec_inputs()

    def _L0_gnn_setup():
        import jax, jax.numpy as jnp
        import numpy as np
        N = 100000
        E = 15625
        D_IN = 128
        D_OUT = 128
        key = jax.random.key(seed)
        ks = jax.random.split(key, 6)
        ego_embedding = jax.random.normal(ks[0], (N, D_IN), dtype=jnp.float32)
        norm = jax.random.uniform(ks[1], (N, 1), dtype=jnp.float32)
        src = jax.random.randint(ks[2], (E,), 0, N, dtype=jnp.int32)
        dst = jax.random.randint(ks[3], (E,), 0, N, dtype=jnp.int32)
        s = 1.0 / np.sqrt(D_IN)
        W1 = jax.random.uniform(ks[4], (D_IN, D_OUT), dtype=jnp.float32, minval=-s, maxval=s)
        W2 = jax.random.uniform(ks[5], (D_IN, D_OUT), dtype=jnp.float32, minval=-s, maxval=s)
        return {'ego_embedding': ego_embedding, 'norm': norm, 'src': src, 'dst': dst, 'W1': W1, 'W2': W2}
    _L0_gnn_all = _L0_gnn_setup()
    _L0_gnn_in = {k: v for k, v in _L0_gnn_all.items() if k in ('W1', 'W2')}
    del _L0_gnn_all
    return {'x': x, 'src': src, 'dst': dst, 'L0_gnn_W1': _L0_gnn_in['W1'], 'L0_gnn_W2': _L0_gnn_in['W2']}

def reference(x, src, dst, L0_gnn_W1, L0_gnn_W2):
    import jax
    import jax.numpy as jnp

    def _L0_gnn_ref(ego_embedding, norm, src, dst, W1, W2):
        import jax, jax.numpy as jnp
        import numpy as np
        N = 100000
        E = 15625
        D_IN = 128
        D_OUT = 128
        h_src = ego_embedding[src]
        h_dst = ego_embedding[dst]
        msg = h_src @ W1 + h_src * h_dst @ W2
        msg = msg * (norm[src] * norm[dst])
        h_N = jax.ops.segment_sum(msg, dst, num_segments=N)
        h_N = h_N + ego_embedding @ W1
        h = jnp.where(h_N >= 0, h_N, 0.2 * h_N)
        nrm = jnp.sqrt(jnp.sum(h * h, axis=1, keepdims=True))
        h = h / jnp.maximum(nrm, 1e-12)
        return h
    deg = jnp.maximum(jax.ops.segment_sum(jnp.ones(dst.shape, jnp.float32), dst, num_segments=100000), 1.0)
    deg_isqrt = deg ** (-0.5)
    h = jnp.maximum(_layernorm(x, axis=-1), 0.0)
    x = x + _L0_gnn_ref(h, deg_isqrt[:, None], src, dst, L0_gnn_W1, L0_gnn_W2)
    return x

_drawn_inputs = setup_inputs


def setup_inputs(seed=0):
    import zlib

    import numpy as np

    out = dict(_drawn_inputs(seed))
    spreads = {}
    factors = {'L0_gnn_W2': 3.703}
    for name, (base, spread) in spreads.items():
        noise = np.random.default_rng([zlib.crc32(name.encode()), seed]).standard_normal(out[name].shape)
        drawn = base * np.exp(spread * noise) if base else spread * noise
        out[name] = jnp.asarray(drawn.astype(out[name].dtype))
    for name, factor in factors.items():
        out[name] = (out[name] * factor).astype(out[name].dtype)
    return out
```

```python
from contextlib import ExitStack

import numpy as np
import concourse.bass as bass
from concourse import mybir

ALU = mybir.AluOpType
ACT = mybir.ActivationFunctionType
AX = mybir.AxisListType
F32 = mybir.dt.float32
F16 = mybir.dt.float16
BF16 = mybir.dt.bfloat16
I32 = mybir.dt.int32

P = 128
D = 128
EPS = 1e-5
NORM_MIN = 1e-12
SLOPE = 0.2

TD = 16
TE = 4
TS = TD + 2 * TE
NQ = TD // 4
BUFS = 4


class Step:

    def __init__(self, blk, r):
        self.blk, self.r = blk, r

    def __call__(self, d=0):
        return self.blk * BUFS + (self.r + d)

    def buf(self, d=0, n=BUFS):
        return (self.r + d) % n

    def dma(self, d=0, per=1):
        return (self.blk + ((self.r + d) // BUFS + 1)) * (16 * per)


def gnn_preln_kernel(nc, x, src, dst, W1, W2, out):
    N = x.shape[0]
    E = src.shape[0]
    CH = P * TD
    STEPS = -(-N // CH)
    G = STEPS * TE
    assert G * P >= E and D == x.shape[1]
    LASTP = (N - (STEPS - 1) * CH) // TD
    assert (STEPS - 1) * CH + LASTP * TD == N
    Q = G // 2
    QW = 2 * P
    QF = E // QW
    QR = E - QF * QW
    assert QF == Q - 1 and 0 < QR < QW
    J = -(-N // P)
    PAD = float(1 << 20)
    LOOPS = (STEPS - 1 - 2) // BUFS

    ntab = nc.dram_tensor("norm_table", [P * J, 1], F32).ap()
    nfd = nc.dram_tensor("same_segment", [Q, QW], BF16).ap()
    flagd = nc.dram_tensor("late_flag", [1, 1], I32).ap()
    lated = nc.dram_tensor("edge_rows", [Q * P, 2 * D], F32).ap()

    with ExitStack() as ctx:
        def sb(name, shape, dt=F32):
            return ctx.enter_context(nc.sbuf_tensor(name, shape, dt))

        def sem(name):
            return ctx.enter_context(nc.semaphore(name))

        def sems(name, n=BUFS):
            return [sem(f"{name}{i}") for i in range(n)]

        ident = sb("ident", [P, P])
        nident = sb("nident", [P, P])
        w1 = sb("w1", [P, D])
        w2 = sb("w2", [P, D])
        eps = sb("eps", [P, 1])
        zero = sb("zero", [P, 1])
        ones = sb("ones", [1, 1])
        xin = sb("xin", [P, BUFS, TD * D])
        ybuf = sb("ybuf", [P, BUFS, TD * D])
        xo = sb("xo", [P, 2, TD * D])
        ct = sb("ct", [P, 2, 4 * D])
        xs = sb("xs", [P, BUFS, TE, D])
        xd = sb("xd", [P, BUFS, TE, D])
        nsrc = sb("nsrc", [P, BUFS, TE])
        same = sb("same", [P, BUFS, TE * P], BF16)
        hs = sb("hs", [P, 2, TE, D])
        hd = sb("hd", [P, 2, TE, D])
        hdt = sb("hdt", [P, 2, TE * P])
        agg = sb("agg", [P, 2, TE * P])
        prod = sb("prod", [P, 2, TE * P])
        u1s = sb("u1s", [P, 2, TE * D])
        ve = sb("ve", [P, TE * D])
        ye = sb("ye", [P, BUFS, TE * D])
        oe = sb("oe", [P, BUFS, TE, D])
        bst = sb("bst", [P, TS, 6])
        msum = sb("msum", [P, TS])
        mdif = sb("mdif", [P, TS])
        m2 = sb("m2", [P, TS])
        dsq = sb("dsq", [P, TS])
        mean = sb("mean", [P, 2, TS])
        var = sb("var", [P, 2, TS])
        guard = sb("guard", [P, BUFS, TD + TE])
        sd = sb("sd", [P, 2 * TE])
        rs = sb("rs", [P, 2, 2 * TE])
        scs = sb("scs", [P, 2, TE])
        bia = sb("bia", [P, 2, 2 * TE])
        ss = sb("ss", [P, BUFS, TD + TE])
        d2 = sb("d2", [P, TD + TE])
        dd = sb("dd", [P, TD + TE])
        rd = sb("rd", [P, TD + TE])
        junk = sb("junk", [P, TD + TE, D], BF16)
        idx = sb("idx", [P, STEPS, 4, 2, 2], I32)
        idl = sb("idl", [P, Q, 2], I32)
        lohi = sb("lohi", [P, 2, Q, 2])
        nd = sb("nd", [P, Q, 2])
        stage = sb("stage", [P, BUFS, 3 * TE], I32)
        sstage = sb("sstage", [P, BUFS, TE], I32)
        lstage = sb("lstage", [P, 2, 2], I32)
        nat = sb("nat", [Q, 5, QW], I32)
        natf = sb("natf", [Q, 8, QW])
        df = sb("df", [Q, QW])
        nf = sb("nf", [Q, QW])
        nl = sb("nl", [Q, QW])
        nf16 = sb("nf16", [Q, QW], BF16)
        cloc = sb("cloc", [Q, QW])
        fsm = sb("fsm", [Q, QW])
        onesq = sb("onesq", [Q, QW])
        iotai = sb("iotai", [P, J], I32)
        iotaf = sb("iotaf", [P, J], F16)
        ioq = sb("ioq", [Q, QW])
        rowi = sb("rowi", [Q, 2], I32)
        lim = sb("lim", [Q, 1])
        endc = sb("endc", [Q, 5])
        rows = sb("rows", [1, 6, P])
        flf = sb("flf", [Q, QW])
        flr = sb("flr", [Q, 1])
        fli = sb("fli", [1, 1], I32)
        lrow = sb("lrow", [P, 2, 2 * D])
        ohl = sb("ohl", [P, BUFS, P], F16)
        ohh = sb("ohh", [P, BUFS, J], F16)
        tabs = xin[:, 0, 0:J]
        tabq = xin[:, 1, 0:J]
        ndq = xin[:, 2, 0:2 * Q]

        pt = ctx.enter_context(nc.psum_tensor("pt", [P, 2, 512], F32))
        pu = ctx.enter_context(nc.psum_tensor("pu", [P, 2, 512], F32))
        pe_s = ctx.enter_context(nc.psum_tensor("pe_s", [P, 512], F32))
        pe_d = ctx.enter_context(nc.psum_tensor("pe_d", [P, 512], F32))
        pe_1 = ctx.enter_context(nc.psum_tensor("pe_1", [P, 512], F32))
        pe_2 = ctx.enter_context(nc.psum_tensor("pe_2", [P, 512], F32))
        turned = [pt[:, 0, :], pt[:, 1, :], pu[:, 0, :], pu[:, 1, :], pe_s[:], pe_d[:], pe_1[:], pe_2[:]]

        s_filled = sem("s_filled")
        s_nat = sem("s_nat")
        s_w = sem("s_w")
        s_zero = sem("s_zero")
        s_ident = sem("s_ident")
        s_iota = sem("s_iota")
        s_const = sem("s_const")
        s_ch = sem("s_ch")
        s_endc = sem("s_endc")
        s_carryrow = sem("s_carryrow")
        s_late = sem("s_late")
        s_ends = sem("s_ends")
        s_carry = sem("s_carry")
        s_natf = sem("s_natf")
        s_turn = sem("s_turn")
        s_idx = sem("s_idx")
        s_cnt = sem("s_cnt")
        s_ndq = sem("s_ndq")
        s_oh = sem("s_oh")
        s_ohu = sem("s_ohu")
        s_tab = sem("s_tab")
        s_tabq = sem("s_tabq")
        s_tabr = sem("s_tabr")
        s_ntab = sem("s_ntab")
        s_nfd = sem("s_nfd")
        s_flag = sem("s_flag")
        s_setup = sem("s_setup")
        x_loaded = sems("x_loaded")
        same_loaded = sems("same_loaded")
        xs_got = sems("xs_got")
        xd_got = sems("xd_got")
        nsrc_got = sems("nsrc_got")
        out_stored = sems("out_stored")
        late_stored = sems("late_stored")
        scattered = sems("scattered")
        staged = sem("staged")
        sstaged = sem("sstaged")
        bn_done = sem("bn_done")
        st_chain = sem("st_chain")
        mean_ready = sem("mean_ready")
        var_ready = sem("var_ready")
        sd_ready = sem("sd_ready")
        rs_chain = sem("rs_chain")
        affine_ready = sem("affine_ready")
        relu_done = sem("relu_done")
        et_done = sem("et_done")
        hdt_done = sem("hdt_done")
        scan_done = sem("scan_done")
        prod_done = sem("prod_done")
        em_done = sem("em_done")
        u1_done = sem("u1_done")
        ve_done = sem("ve_done")
        ye_done = sem("ye_done")
        t_done = sem("t_done")
        t_evac = sem("t_evac")
        m_done = sem("m_done")
        u_evac = sem("u_evac")
        y_done = sem("y_done")
        ss_done = sem("ss_done")
        d2_ready = sem("d2_ready")
        dd_ready = sem("dd_ready")
        rd_ready = sem("rd_ready")
        f_done = sem("f_done")
        late_got = sems("late_got", 2)
        late_put = sem("late_put")
        lstaged = sem("lstaged")

        def steps(eng, do, first, last):
            for i in range(first, 2 + BUFS):
                do(Step(i // BUFS, i % BUFS), i)
            with eng.Fori(1, LOOPS) as blk:
                for r in range(2, 2 + BUFS):
                    do(Step(blk + r // BUFS, r % BUFS), None)
            for i in range(LOOPS * BUFS + 2, last + 1):
                do(Step(i // BUFS, i % BUFS), i)

        def has(i, d):
            return i is None or 0 <= i + d < STEPS

        def chunk(t, s, i, d):
            if i is not None and i + d == STEPS - 1:
                return t[(STEPS - 1) * CH:N, :].rearrange("(p t) f -> p (t f)", t=TD), LASTP
            return t[bass.ds(s(d) * CH, CH), :].rearrange("(p t) f -> p (t f)", t=TD), P

        block = ctx.enter_context(nc.Block())

        @block.sync
        def _(sp):
            sp.dma_start(w1[:], W1).then_inc(s_w, 16)
            sp.dma_start(w2[:], W2).then_inc(s_w, 16)
            sp.wait_ge(s_filled, 1)
            flat = lambda t, a, b, q: t[a:b].rearrange("(q w) -> q w", q=q)
            sp.dma_start(nat[0:QF, 0, :], flat(dst, 0, QF * QW, QF)).then_inc(s_nat, 16)
            sp.dma_start(nat[QF:Q, 0, 0:QR], flat(dst, QF * QW, E, 1)).then_inc(s_nat, 16)
            sp.dma_start(nat[0:1, 1, 1:QW], flat(dst, 0, QW - 1, 1)).then_inc(s_nat, 16)
            sp.dma_start(nat[1:QF, 1, :], flat(dst, QW - 1, QF * QW - 1, QF - 1)).then_inc(s_nat, 16)
            sp.dma_start(nat[QF:Q, 1, 0:QR + 1], flat(dst, QF * QW - 1, E, 1)).then_inc(s_nat, 16)
            sp.dma_start(nat[0:QF, 2, :], flat(dst, 1, QF * QW + 1, QF)).then_inc(s_nat, 16)
            sp.dma_start(nat[QF:Q, 2, 0:QR - 1], flat(dst, QF * QW + 1, E, 1)).then_inc(s_nat, 16)
            sp.dma_start(nat[0:QF, 3, :], flat(src, 0, QF * QW, QF)).then_inc(s_nat, 16)
            sp.dma_start(nat[QF:Q, 3, 0:QR], flat(src, QF * QW, E, 1)).then_inc(s_nat, 16)
            sp.wait_ge(s_natf, 1)
            sp.dma_start(nfd, nf16[:]).then_inc(s_nfd, 16)
            sp.wait_ge(s_late, 1)
            sp.dma_start(flagd, fli[:]).then_inc(s_flag, 16)
            sp.wait_ge(s_tabr, 1)
            sp.dma_start(ntab.rearrange("(p j) o -> p (j o)", p=P), tabs).then_inc(s_ntab, 16)
            sp.wait_ge(s_nfd, 16)
            sp.wait_ge(s_ntab, 16)
            sp.wait_ge(s_setup, 1)
            same_flat = nfd.rearrange("q w -> (q w)")

            def do(s, i):
                if has(i, 0):
                    if has(i, -4):
                        sp.wait_ge(f_done, s(-3))
                    src_rows, np_ = chunk(x, s, i, 0)
                    sp.dma_start(xin[0:np_, s.buf(), :], src_rows).then_inc(x_loaded[s.buf()], 16)
                    sp.dma_start(
                        same[:, s.buf(), :],
                        same_flat[bass.ds(s() * (TE * P), TE * P)].rearrange("(o w) -> o w", o=1).to_broadcast([P, TE * P]),
                    ).then_inc(same_loaded[s.buf()], 16)
                if has(i, -3):
                    sp.wait_ge(f_done, s(-2))
                    dst_rows, np_ = chunk(out, s, i, -3)
                    sp.dma_start(dst_rows, xo[0:np_, s.buf(-3, 2), :]).then_inc(out_stored[s.buf(-3)], 16)
                    sp.dma_start(lated[bass.ds(s(-3) * (2 * P), 2 * P), :].rearrange("(h p) w -> p h w", h=2),
                                 oe[:, s.buf(-3), :, :].rearrange("p (h t) f -> p h (t f)", h=2)
                                 ).then_inc(late_stored[s.buf(-3)], 16)

            steps(sp, do, 0, STEPS + 2)
            for b in range(BUFS):
                n = len(range(b, STEPS, BUFS))
                sp.wait_ge(out_stored[b], 16 * n)
                sp.wait_ge(late_stored[b], 16 * n)

        @block.gpsimd
        def _(pool):
            pool.memset(ident[:], 0.0).then_inc(s_zero, 1)
            pool.iota(iotai[:], pattern=[[1, J]], base=0, channel_multiplier=0)
            pool.iota(rowi[:, 0:1], pattern=[[0, 1]], base=0, channel_multiplier=1).then_inc(s_iota, 1)
            pool.wait_ge(s_zero, 1)
            pool.affine_select(out=ident[:], in_=ident[:], compare_op=ALU.not_equal, fill=1.0, base=0,
                               pattern=[[-1, P]], channel_multiplier=1).then_inc(s_ident, 1)
            pool.wait_ge(s_idx, 1)
            row_limit = pool.to_reg(N - 1)
            tab_limit = pool.to_reg(P * J - 1)

            def gather(to, rows, index, limit, done):
                pool.indirect_dma_start(out=to, out_offset=None, in_=rows,
                                        in_offset=bass.IndirectOffsetOnAxis(ap=index, axis=0),
                                        bounds_check=limit, oob_is_err=False).then_inc(done, 16)

            def scatter(rows, index, done):
                pool.indirect_dma_start(out=out, out_offset=bass.IndirectOffsetOnAxis(ap=index, axis=0),
                                        in_=rows, in_offset=None,
                                        bounds_check=row_limit, oob_is_err=False).then_inc(done, 16)

            def stage_gather(s, d):
                pool.tensor_copy(stage[:, s.buf(d), :],
                                 idx[:, bass.ds(s(d), 1), 0:3, :, :].rearrange("p o a q h -> p (o a q h)")
                                 ).then_inc(staged, 1)

            def stage_scatter(s, d):
                pool.tensor_copy(sstage[:, s.buf(d), :],
                                 idx[:, bass.ds(s(d), 1), 3:4, :, :].rearrange("p o a q h -> p (o a q h)")
                                 ).then_inc(sstaged, 1)

            stage_gather(Step(0, 0), 0)
            stage_scatter(Step(0, 0), 0)

            def do(s, i):
                if has(i, 0):
                    b = s.buf()
                    if has(i, -4):
                        pool.wait_ge(relu_done, s(-3))
                        pool.wait_ge(f_done, s(-3))
                    if has(i, -3):
                        pool.wait_ge(xs_got[s.buf(-3)], s.dma(-3, TE))
                        pool.wait_ge(xd_got[s.buf(-3)], s.dma(-3, TE))
                        pool.wait_ge(nsrc_got[s.buf(-3)], s.dma(-3, TE))
                    pool.wait_ge(staged, s(1))
                    if has(i, 1):
                        stage_gather(s, 1)
                    for k in range(TE):
                        gather(xs[:, b, k, :], x, stage[:, b, k:k + 1], row_limit, xs_got[b])
                    for k in range(TE):
                        gather(xd[:, b, k, :], x, stage[:, b, TE + k:TE + k + 1], row_limit, xd_got[b])
                    if i == 0:
                        pool.wait_ge(s_ntab, 16)
                    for k in range(TE):
                        gather(nsrc[:, b, k:k + 1], ntab, stage[:, b, 2 * TE + k:2 * TE + k + 1], tab_limit,
                               nsrc_got[b])
                if has(i, -4):
                    b = s.buf(-4)
                    pool.wait_ge(f_done, s(-3))
                    pool.wait_ge(out_stored[b], s.dma(-4))
                    if has(i, -5):
                        pool.wait_ge(out_stored[s.buf(-5)], s.dma(-5))
                    if has(i, -7):
                        pool.wait_ge(scattered[s.buf(-7)], s.dma(-7, TE))
                    pool.wait_ge(sstaged, s(-3))
                    if has(i, -3):
                        stage_scatter(s, -3)
                    for k in range(TE):
                        scatter(oe[:, b, k, :], sstage[:, b, k:k + 1], scattered[b])

            steps(pool, do, 0, STEPS + 3)
            for b in range(BUFS):
                n = len(range(b, STEPS, BUFS))
                pool.wait_ge(scattered[b], 16 * TE * n)
                pool.wait_ge(out_stored[b], 16 * n)
                pool.wait_ge(late_stored[b], 16 * n)
            pool.wait_ge(s_flag, 16)
            late = pool.value_load(flagd, min_val=0, max_val=1)
            with pool.If(late > 0):
                def bring(q, b):
                    pool.tensor_copy(lstage[:, b, :], idl[:, bass.ds(q, 1), :].rearrange("p o h -> p (o h)")
                                     ).then_inc(lstaged, 1)
                    pool.dma_start(lrow[:, b, :], lated[bass.ds(q * P, P), :]).then_inc(late_got[b], 16)

                def put(q, b, times, first=False, last=False):
                    pool.wait_ge(late_got[b], times * 16 + 16)
                    if not first:
                        pool.wait_ge(late_put, q * 32)
                    pool.wait_ge(lstaged, q + 1)
                    if not last:
                        bring(q + 1, 1 - b)
                    for h in range(2):
                        scatter(lrow[:, b, h * D:(h + 1) * D], lstage[:, b, h:h + 1], late_put)

                bring(0, 0)
                put(0, 0, 0, first=True)
                with pool.Fori(0, Q // 2 - 1) as half:
                    put(half * 2 + 1, 1, half)
                    put(half * 2 + 2, 0, half + 1)
                put(Q - 1, 1, Q // 2 - 1, last=True)
                pool.wait_ge(late_put, 32 * Q)
            pool.nop()

        @block.vector
        def _(dve):
            link = [0]

            def chain(ins):
                link[0] += 1
                ins.then_inc(s_ch, 1)
                dve.wait_ge(s_ch, link[0])

            dve.memset(nat[:, 0, :], int(PAD))
            dve.memset(nat[:, 1:3, :], -1)
            dve.memset(nat[:, 3, :], 0).then_inc(s_filled, 1)
            dve.memset(eps[:], EPS)
            dve.memset(zero[:], 0.0)
            dve.memset(ones[:], 1.0)
            dve.memset(rows[:], 0.0)
            dve.memset(onesq[:], 1.0)
            dve.memset(guard[:], NORM_MIN * NORM_MIN)
            dve.wait_ge(s_iota, 1)
            dve.tensor_copy(iotaf[:], iotai[:])
            dve.tensor_scalar(ioq[:], iotai[0:Q, 0:QW], 1.0, None, ALU.add)
            chain(dve.tensor_scalar(rowi[:, 1:2], rowi[:, 0:1], 1, None, ALU.logical_shift_right))
            dve.tensor_scalar(lim[:], rowi[:, 1:2], float(CH), float(CH - 1), ALU.mult, ALU.add)
            dve.wait_ge(s_ident, 1)
            dve.tensor_scalar(nident[:], ident[:], -1.0, None, ALU.mult).then_inc(s_const, 1)
            dve.wait_ge(s_nat, 16 * 9)
            chain(dve.tensor_scalar(nat[:, 4, :], nat[:, 0, :], P - 1, None, ALU.bitwise_and))
            chain(dve.tensor_copy(natf[:, 5, :], nat[:, 4, :]))
            chain(dve.tensor_scalar(nat[:, 4, :], nat[:, 0, :], 7, None, ALU.logical_shift_right))
            chain(dve.tensor_copy(natf[:, 6, :], nat[:, 4, :]))
            chain(dve.tensor_scalar(nat[:, 4, :], nat[:, 3, :], P - 1, None, ALU.bitwise_and))
            dve.tensor_copy(natf[:, 0, :], nat[:, 3, :])
            chain(dve.tensor_copy(cloc[:], nat[:, 4, :]))
            chain(dve.tensor_scalar(nat[:, 4, :], nat[:, 3, :], 7, None, ALU.logical_shift_right))
            chain(dve.tensor_copy(fsm[:], nat[:, 4, :]))
            dve.scalar_tensor_tensor(natf[:, 2, :], cloc[:], float(J), fsm[:], ALU.mult, ALU.add)
            chain(dve.tensor_copy(df[:], nat[:, 0, :]))
            dve.tensor_scalar(natf[:, 1, :], df[:], float(N - 1), None, ALU.min)
            chain(dve.tensor_tensor(nf[:], nat[:, 0, :], nat[:, 1, :], ALU.is_equal))
            dve.tensor_tensor(nl[:], nat[:, 0, :], nat[:, 2, :], ALU.is_equal)
            dve.tensor_copy(nf16[:], nf[:])
            chain(dve.tensor_tensor_scan(cloc[:], nf[:], onesq[:], 0.0, ALU.mult, ALU.add))
            dve.tensor_copy(endc[:, 0:1], cloc[:, QW - 1:QW])
            dve.tensor_copy(endc[:, 2:3], nf[:, 0:1])
            dve.scalar_tensor_tensor(endc[:, 1:2], cloc[:, QW - 1:QW], float(QW), nf[:, 0:1],
                                     ALU.is_equal, ALU.mult)
            chain(dve.tensor_tensor(fsm[:], cloc[:], ioq[:], ALU.is_equal))
            chain(dve.tensor_scalar(flf[:], df[:], lim[:, 0:1], None, ALU.is_gt))
            chain(dve.tensor_tensor(natf[:, 7, :], flf[:], nl[:], ALU.max))
            chain(dve.scalar_tensor_tensor(natf[:, 3, :], natf[:, 7, :], PAD, df[:], ALU.mult, ALU.add))
            chain(dve.tensor_scalar(natf[:, 7, :], flf[:], -1.0, 1.0, ALU.mult, ALU.add))
            chain(dve.tensor_tensor(flf[:], natf[:, 7, :], nl[:], ALU.max))
            chain(dve.scalar_tensor_tensor(natf[:, 4, :], flf[:], PAD, df[:], ALU.mult, ALU.add))
            chain(dve.tensor_scalar(flf[:], natf[:, 4, :], float(N), None, ALU.is_lt))
            chain(dve.tensor_reduce(endc[:, 4:5], flf[:], AX.X, ALU.max))
            dve.tensor_copy(endc[:, 3:4], endc[:, 0:1]).then_inc(s_endc, 1)
            dve.wait_ge(s_ends, 1)
            for k in range(3):
                dve.tensor_copy(rows[0:1, k, 0:Q], pe_s[0:1, k * P:k * P + Q])
            chain(dve.tensor_reduce(rows[0:1, 5, 0:1], pe_s[0:1, 3 * P:3 * P + Q], AX.X, ALU.max))
            dve.tensor_copy(fli[:], rows[0:1, 5, 0:1]).then_inc(s_late, 1)
            chain(dve.tensor_tensor_scan(rows[0:1, 3, 0:Q], rows[0:1, 1, 0:Q], rows[0:1, 0, 0:Q], 0.0,
                                         ALU.mult, ALU.add))
            dve.tensor_tensor(rows[0:1, 4, 1:Q], rows[0:1, 2, 1:Q], rows[0:1, 3, 0:Q - 1], ALU.mult).then_inc(s_carryrow, 1)
            dve.wait_ge(s_carry, 1)
            chain(dve.tensor_copy(flr[:], pe_d[0:Q, 0:1]))
            dve.scalar_tensor_tensor(natf[:, 7, :], fsm[:], flr[:, 0:1], cloc[:], ALU.mult, ALU.add
                                     ).then_inc(s_natf, 1)
            dve.wait_ge(s_turn, 1)
            for h in range(2):
                for a in range(8):
                    col = turned[a][:, h * P:h * P + Q]
                    if a < 4:
                        dve.tensor_copy(idx[:, :, a, :, h], col.rearrange("p (b q) -> p b q", q=2))
                    elif a == 4:
                        dve.tensor_copy(idl[:, :, h], col)
                    elif a < 7:
                        dve.tensor_copy(lohi[:, a - 5, :, h], col)
                    else:
                        last = dve.tensor_copy(nd[:, :, h], col)
                    if (h, a) == (1, 6):
                        pass
            last.then_inc(s_idx, 1)
            dve.wait_ge(s_idx, 1)
            dve.wait_ge(s_ndq, 1)
            dve.reciprocal(nd[:].rearrange("p q h -> p (q h)"), ndq)
            col = lohi[:].rearrange("p a q h -> p a (q h)")

            def onehot(g, k, wait):
                if wait:
                    dve.wait_ge(s_ohu, g - (BUFS - 1))
                dve.tensor_scalar(ohl[:, k, :], iotaf[:, 0:P], col[:, 0, bass.ds(g, 1)], None, ALU.is_equal)
                dve.tensor_scalar(ohh[:, k, :], iotaf[:], col[:, 1, bass.ds(g, 1)], None, ALU.is_equal
                                  ).then_inc(s_oh, 1)

            for k in range(BUFS):
                onehot(k, k, False)
            with dve.Fori(1, G // BUFS) as b:
                for k in range(BUFS):
                    onehot(b * BUFS + k, k, True)
            dve.wait_ge(s_ohu, G)
            dve.tensor_scalar(tabs[:, 0:512], pt[:, 0, :], 1.0, None, ALU.max)
            dve.tensor_scalar(tabs[:, 512:J], pt[:, 1, 0:J - 512], 1.0, None, ALU.max).then_inc(s_tab, 1)
            dve.wait_ge(s_tabq, 1)
            dve.reciprocal(tabs, tabq).then_inc(s_tabr, 1)
            dve.wait_ge(s_tabr, 1)
            dve.memset(zero[:], 0.0).then_inc(s_setup, 1)

            def do(s, i):
                if has(i, 0):
                    b, h = s.buf(), s.buf(0, 2)
                    dve.wait_ge(x_loaded[b], s.dma())
                    for t in range(TD):
                        dve.bn_stats(bst[:, t, :], xin[:, b, t * D:(t + 1) * D])
                    dve.wait_ge(xs_got[b], s.dma(0, TE))
                    for t in range(TE):
                        dve.bn_stats(bst[:, TD + t, :], xs[:, b, t, :])
                    dve.wait_ge(xd_got[b], s.dma(0, TE))
                    for t in range(TE):
                        last = dve.bn_stats(bst[:, TD + TE + t, :], xd[:, b, t, :])
                    last.then_inc(bn_done, 1)
                if has(i, -2):
                    dve.wait_ge(ss_done, s(-1))
                    dve.tensor_tensor(d2[:], ss[:, s.buf(-2), :], guard[:, s.buf(-2), :], ALU.max).then_inc(d2_ready, 1)
                if has(i, 0):
                    dve.wait_ge(bn_done, s(1))
                    dve.tensor_tensor(msum[:], bst[:, :, 1], bst[:, :, 4], ALU.add)
                    dve.tensor_tensor(mdif[:], bst[:, :, 1], bst[:, :, 4], ALU.subtract)
                    dve.tensor_tensor(m2[:], bst[:, :, 2], bst[:, :, 5], ALU.add).then_inc(st_chain, 1)
                    dve.wait_ge(st_chain, s() * 2 + 1)
                    dve.tensor_scalar(mean[:, h, :], msum[:], 0.5, None, ALU.mult).then_inc(mean_ready, 1)
                    dve.scalar_tensor_tensor(dsq[:], mdif[:], 0.25, mdif[:], ALU.mult, ALU.mult).then_inc(st_chain, 1)
                    dve.wait_ge(st_chain, s() * 2 + 2)
                    dve.scalar_tensor_tensor(var[:, h, :], m2[:], 1.0 / D, dsq[:], ALU.mult, ALU.add
                                             ).then_inc(var_ready, 1)
                if has(i, -1):
                    b, h, hp = s.buf(-1), s.buf(-1, 2), s.buf(-2, 2)
                    dve.wait_ge(et_done, s())
                    dve.wait_ge(same_loaded[b], s.dma(-1))
                    if has(i, -3):
                        dve.wait_ge(em_done, s(-2))
                    if i == 1:
                        start = 0.0
                    else:
                        dve.wait_ge(scan_done, s(-1))
                        start = agg[:, hp, TE * P - 1:TE * P]
                    dve.tensor_tensor_scan(agg[:, h, :], same[:, b, :], pe_s[:], start, ALU.mult, ALU.add
                                           ).then_inc(scan_done, 1)
                    dve.wait_ge(scan_done, s())
                    dve.wait_ge(hdt_done, s())
                    dve.tensor_tensor(prod[:, h, :], agg[:, h, :], hdt[:, h, :], ALU.mult).then_inc(prod_done, 1)
                if has(i, 0):
                    b, h = s.buf(), s.buf(0, 2)
                    dve.wait_ge(var_ready, s(1))
                    dve.tensor_scalar(guard[:, b, 0:TD], var[:, h, 0:TD], EPS, NORM_MIN * NORM_MIN, ALU.add, ALU.mult)
                    dve.wait_ge(sd_ready, s(1))
                    if has(i, -2):
                        dve.wait_ge(relu_done, s(-1))
                    dve.reciprocal(rs[:, h, :], sd[:]).then_inc(rs_chain, 1)
                    dve.wait_ge(nsrc_got[b], s.dma(0, TE))
                    dve.wait_ge(rs_chain, s() * 2 + 1)
                    dve.scalar_tensor_tensor(bia[:, h, TE:2 * TE], mean[:, h, TD + TE:TS], -1.0, rs[:, h, TE:2 * TE],
                                             ALU.mult, ALU.mult)
                    dve.tensor_tensor(scs[:, h, :], rs[:, h, 0:TE], nsrc[:, b, :], ALU.mult).then_inc(rs_chain, 1)
                    dve.wait_ge(rs_chain, s() * 2 + 2)
                    dve.scalar_tensor_tensor(bia[:, h, 0:TE], mean[:, h, TD:TD + TE], -1.0, scs[:, h, :],
                                             ALU.mult, ALU.mult).then_inc(affine_ready, 1)
                if has(i, -2):
                    dve.wait_ge(dd_ready, s(-1))
                    dve.reciprocal(rd[:], dd[:]).then_inc(rd_ready, 1)
                if has(i, -1):
                    yb = ybuf[:, s.buf(-1), :]
                    dve.wait_ge(u_evac, s() * NQ)
                    dve.scalar_tensor_tensor(yb, yb, SLOPE, yb, ALU.mult, ALU.max).then_inc(y_done, 1)
                if has(i, -2):
                    b = s.buf(-2)
                    dve.wait_ge(rd_ready, s(-1))
                    if has(i, -6):
                        dve.wait_ge(scattered[b], s.dma(-6, TE))
                        dve.wait_ge(late_stored[b], s.dma(-6))
                    for t in range(TE):
                        dve.scalar_tensor_tensor(oe[:, b, t, :], ye[:, b, t * D:(t + 1) * D], rd[:, TD + t:TD + t + 1],
                                                 xd[:, b, t, :], ALU.mult, ALU.add)
                    if has(i, -4):
                        dve.wait_ge(out_stored[s.buf(-4)], s.dma(-4))
                    for t in range(TD):
                        f = slice(t * D, (t + 1) * D)
                        last = dve.scalar_tensor_tensor(xo[:, s.buf(-2, 2), f], ybuf[:, b, f], rd[:, t:t + 1],
                                                        xin[:, b, f], ALU.mult, ALU.add)
                    last.then_inc(f_done, 1)
                if has(i, -1):
                    h = s.buf(-1, 2)
                    dve.wait_ge(em_done, s())
                    dve.wait_ge(u1_done, s())
                    ndf = nd[:].rearrange("p q h -> p (q h)")
                    for t in range(TE):
                        f = slice(t * D, (t + 1) * D)
                        last = dve.scalar_tensor_tensor(ve[:, f], pe_2[:, f], ndf[:, bass.ds(s(-1) * TE + t, 1)],
                                                        u1s[:, h, f], ALU.mult, ALU.add)
                    last.then_inc(ve_done, 1)
                    dve.wait_ge(ve_done, s())
                    dve.scalar_tensor_tensor(ye[:, s.buf(-1), :], ve[:], SLOPE, ve[:], ALU.mult, ALU.max
                                             ).then_inc(ye_done, 1)

            steps(dve, do, 0, STEPS + 1)

        @block.scalar
        def _(act):
            act.wait_ge(s_idx, 1)
            act.activation(ndq, nd[:].rearrange("p q h -> p (q h)"), ACT.Sqrt).then_inc(s_ndq, 1)
            act.wait_ge(s_tab, 1)
            act.activation(tabq, tabs, ACT.Sqrt).then_inc(s_tabq, 1)

            def do(s, i):
                if has(i, -2):
                    b = s.buf(-2)
                    act.wait_ge(ye_done, s(-1))
                    for t in range(TE):
                        last = act.activation(junk[:, TD + t, :], ye[:, b, t * D:(t + 1) * D], ACT.Square,
                                              accum_out=ss[:, b, TD + t:TD + t + 1])
                    last.then_inc(ss_done, 1)
                if has(i, -1):
                    act.wait_ge(et_done, s())
                    if has(i, -3):
                        act.wait_ge(em_done, s(-2))
                    act.copy(hdt[:, s.buf(-1, 2), :], pe_d[:]).then_inc(hdt_done, 1)
                if has(i, 0):
                    act.wait_ge(var_ready, s(1))
                    if has(i, -1):
                        act.wait_ge(affine_ready, s())
                    act.activation(sd[:], var[:, s.buf(0, 2), TD:TS], ACT.Sqrt, bias=eps[:, 0:1]).then_inc(sd_ready, 1)

                def relu_quarter(q):
                    act.wait_ge(t_done, s() * NQ + (q + 1))
                    if q >= 2 or has(i, -1):
                        act.wait_ge(m_done, s() * NQ + (q - 1))
                    act.activation(ct[:, q % 2, :], pt[:, q % 2, :], ACT.Relu).then_inc(t_evac, 1)

                def copy_quarter(q):
                    act.wait_ge(m_done, s() * NQ + (q + 1))
                    act.copy(ybuf[:, s.buf(), q * 512:(q + 1) * 512], pu[:, q % 2, :]).then_inc(u_evac, 1)

                if has(i, 0):
                    relu_quarter(0)
                    relu_quarter(1)
                if has(i, -2):
                    act.wait_ge(d2_ready, s(-1))
                    if has(i, -3):
                        act.wait_ge(rd_ready, s(-2))
                    act.activation(dd[:], d2[:], ACT.Sqrt).then_inc(dd_ready, 1)
                if has(i, 0):
                    if has(i, -4):
                        act.wait_ge(f_done, s(-3))
                    copy_quarter(0)
                    relu_quarter(2)
                    copy_quarter(1)
                if has(i, -1):
                    act.wait_ge(em_done, s())
                    if has(i, -3):
                        act.wait_ge(ve_done, s(-2))
                    act.copy(u1s[:, s.buf(-1, 2), :], pe_1[:]).then_inc(u1_done, 1)
                if has(i, 0):
                    relu_quarter(3)
                    copy_quarter(2)
                    copy_quarter(3)
                    b, h = s.buf(), s.buf(0, 2)
                    act.wait_ge(affine_ready, s(1))
                    if has(i, -2):
                        act.wait_ge(et_done, s(-1))
                    for t in range(TE):
                        act.activation(hs[:, h, t, :], xs[:, b, t, :], ACT.Relu, bias=bia[:, h, t:t + 1],
                                       scale=scs[:, h, t:t + 1])
                    for t in range(TE):
                        last = act.activation(hd[:, h, t, :], xd[:, b, t, :], ACT.Relu,
                                              bias=bia[:, h, TE + t:TE + t + 1], scale=rs[:, h, TE + t:TE + t + 1])
                    last.then_inc(relu_done, 1)
                if has(i, -1):
                    b = s.buf(-1)
                    act.wait_ge(y_done, s())
                    for t in range(TD):
                        act.activation(junk[:, t, :], ybuf[:, b, t * D:(t + 1) * D], ACT.Square,
                                       accum_out=ss[:, b, t:t + 1])

            steps(act, do, 0, STEPS + 1)

        @block.tensor
        def _(pe):
            pe.wait_ge(s_const, 1)
            pe.wait_ge(s_endc, 1)
            for k, c in enumerate((0, 1, 2, 4)):
                last = pe.matmul(pe_s[0:1, k * P:k * P + Q], endc[:, c:c + 1], ident[0:Q, 0:Q], start=True, stop=True)
            last.then_inc(s_ends, 1)
            pe.wait_ge(s_carryrow, 1)
            pe.matmul(pe_d[0:Q, 0:1], rows[0:1, 4, 0:Q], ones[0:1, 0:1], start=True, stop=True).then_inc(s_carry, 1)
            pe.wait_ge(s_natf, 1)
            for a in range(8):
                for h in range(2):
                    last = pe.transpose(turned[a][:, h * P:h * P + Q], natf[:, a, h * P:(h + 1) * P], ident[0:Q, 0:Q])
            last.then_inc(s_turn, 1)
            pe.wait_ge(s_idx, 1)

            def count(g, k, first, final):
                pe.wait_ge(s_oh, g + 1)
                pe.matmul(pt[:, 0, :], ohl[:, k, :], ohh[:, k, 0:512], start=first, stop=final)
                pe.matmul(pt[:, 1, 0:J - 512], ohl[:, k, :], ohh[:, k, 512:J], start=first, stop=final
                          ).then_inc(s_ohu, 1)

            for k in range(BUFS):
                count(k, k, k == 0, False)
            with pe.Fori(1, G // BUFS - 1) as b:
                for k in range(BUFS):
                    count(b * BUFS + k, k, False, False)
            for k in range(BUFS):
                count(G - BUFS + k, k, False, k == BUFS - 1)
            pe.wait_ge(s_tab, 1)
            pe.wait_ge(s_w, 32)

            def do(s, i):
                def turn_quarter(q):
                    if q >= 2 or has(i, -1):
                        pe.wait_ge(t_evac, s() * NQ + (q - 1))
                    for t in range(4):
                        f = slice(t * D, (t + 1) * D)
                        col = q * 4 + t
                        pe.matmul(pt[:, q % 2, f], xin[:, s.buf(), col * D:(col + 1) * D], ident[:],
                                  is_transpose=True, start=True, stop=False)
                        last = pe.matmul(pt[:, q % 2, f], mean[:, s.buf(0, 2), col:col + 1].to_broadcast([P, D]),
                                         nident[:], start=False, stop=True)
                    last.then_inc(t_done, 1)

                def mul_quarter(q):
                    pe.wait_ge(t_evac, s() * NQ + (q + 1))
                    if q >= 2 or has(i, -1):
                        pe.wait_ge(u_evac, s() * NQ + (q - 1))
                    for t in range(4):
                        f = slice(t * D, (t + 1) * D)
                        last = pe.matmul(pu[:, q % 2, f], ct[:, q % 2, f], w1[:], start=True, stop=True)
                    last.then_inc(m_done, 1)

                if has(i, 0):
                    pe.wait_ge(mean_ready, s(1))
                    turn_quarter(0)
                    turn_quarter(1)
                    mul_quarter(0)
                    turn_quarter(2)
                    mul_quarter(1)
                if has(i, -1):
                    h = s.buf(-1, 2)
                    pe.wait_ge(hdt_done, s())
                    pe.wait_ge(prod_done, s())
                    if has(i, -2):
                        pe.wait_ge(u1_done, s(-1))
                        pe.wait_ge(ve_done, s(-1))
                    for t in range(TE):
                        f = slice(t * D, (t + 1) * D)
                        pe.matmul(pe_1[:, f], hdt[:, h, f], w1[:], start=True, stop=True)
                        pe.matmul(pe_2[:, f], agg[:, h, f], w1[:], start=True, stop=False)
                        last = pe.matmul(pe_2[:, f], prod[:, h, f], w2[:], start=False, stop=True)
                    last.then_inc(em_done, 1)
                if has(i, 0):
                    turn_quarter(3)
                    mul_quarter(2)
                    mul_quarter(3)
                    h = s.buf(0, 2)
                    pe.wait_ge(relu_done, s(1))
                    if has(i, -1):
                        pe.wait_ge(prod_done, s())
                        pe.wait_ge(hdt_done, s())
                    for t in range(TE):
                        f = slice(t * D, (t + 1) * D)
                        pe.transpose(pe_s[:, f], hs[:, h, t, :], ident[:])
                        last = pe.transpose(pe_d[:, f], hd[:, h, t, :], ident[:])
                    last.then_inc(et_done, 1)

            steps(pe, do, 0, STEPS)


def kernel(**inputs):
    import concourse.bacc as bacc
    from concourse.bass_utils import run_bass_kernel_spmd

    nc = bacc.Bacc("TRN2", target_bir_lowering=False, num_devices=1)
    arrays, args = {}, []
    for name in ("x", "src", "dst", "L0_gnn_W1", "L0_gnn_W2"):
        a = np.ascontiguousarray(inputs[name])
        arrays[f"in_{name}"] = a
        args.append(nc.dram_tensor(f"in_{name}", a.shape, mybir.dt.from_np(a.dtype), kind="ExternalInput").ap())
    out = nc.dram_tensor("out", arrays["in_x"].shape, F32, kind="ExternalOutput").ap()
    gnn_preln_kernel(nc, *args, out)
    r = run_bass_kernel_spmd(nc, [arrays], core_ids=[0])
    return r.results[0]["out"]
```

```python
from contextlib import ExitStack

import numpy as np
import concourse.bass as bass
from concourse import mybir

ALU = mybir.AluOpType
ACT = mybir.ActivationFunctionType
AX = mybir.AxisListType
F32 = mybir.dt.float32
F16 = mybir.dt.float16
BF16 = mybir.dt.bfloat16
I32 = mybir.dt.int32

P = 128
D = 128
EPS = 1e-5
NORM_MIN = 1e-12
SLOPE = 0.2

TD = 16
TE = 4
TS = TD + 2 * TE
NQ = TD // 4
BUFS = 4
XBUFS = 8
UN = 8


class Step:

    def __init__(self, blk, r):
        self.blk, self.r = blk, r

    def __call__(self, d=0):
        return self.blk * UN + (self.r + d)

    def buf(self, d=0, n=BUFS):
        return (self.r + d) % n

    def dma(self, d=0, per=1, n=BUFS):
        return (self.blk * (UN // n) + ((self.r + d) // n + 1)) * (16 * per)


def gnn_preln_kernel(nc, x, src, dst, W1, W2, out):
    N = x.shape[0]
    E = src.shape[0]
    CH = P * TD
    STEPS = -(-N // CH)
    G = STEPS * TE
    assert G * P >= E and D == x.shape[1]
    LASTP = (N - (STEPS - 1) * CH) // TD
    assert (STEPS - 1) * CH + LASTP * TD == N
    Q = G // 2
    QW = 2 * P
    QF = E // QW
    QR = E - QF * QW
    assert QF == Q - 1 and 0 < QR < QW
    J = -(-N // P)
    PAD = float(1 << 20)
    AHEAD = 5
    LOOPS = (STEPS - AHEAD) // UN

    ntab = nc.dram_tensor("norm_table", [P * J, 1], F32).ap()
    nfd = nc.dram_tensor("same_segment", [Q, QW], BF16).ap()
    flagd = nc.dram_tensor("late_flag", [1, 1], I32).ap()
    lated = nc.dram_tensor("edge_rows", [Q * P, 2 * D], F32).ap()

    with ExitStack() as ctx:
        def sb(name, shape, dt=F32):
            return ctx.enter_context(nc.sbuf_tensor(name, shape, dt))

        def sem(name):
            return ctx.enter_context(nc.semaphore(name))

        def sems(name, n=BUFS):
            return [sem(f"{name}{i}") for i in range(n)]

        ident = sb("ident", [P, P])
        nident = sb("nident", [P, P])
        w1 = sb("w1", [P, D])
        w2 = sb("w2", [P, D])
        eps = sb("eps", [P, 1])
        zero = sb("zero", [P, 1])
        ones = sb("ones", [1, 1])
        xin = sb("xin", [P, BUFS, TD * D])
        ybuf = sb("ybuf", [P, BUFS, TD * D])
        xo = sb("xo", [P, 2, TD * D])
        ct = sb("ct", [P, 2, 4 * D])
        xs = sb("xs", [P, XBUFS, TE, D])
        xd = sb("xd", [P, XBUFS, TE, D])
        nsrc = sb("nsrc", [P, XBUFS, TE])
        same = sb("same", [P, BUFS, TE * P], BF16)
        hs = sb("hs", [P, 2, TE, D])
        hd = sb("hd", [P, 2, TE, D])
        hdt = sb("hdt", [P, 2, TE * P])
        agg = sb("agg", [P, 2, TE * P])
        prod = sb("prod", [P, 2, TE * P])
        msg = sb("msg", [P, 2, TE * D])
        ye = sb("ye", [P, BUFS, TE * D])
        oe = sb("oe", [P, BUFS, TE, D])
        bst = sb("bst", [P, TS, 6])
        msum = sb("msum", [P, TS])
        mdif = sb("mdif", [P, TS])
        m2 = sb("m2", [P, TS])
        dsq = sb("dsq", [P, TS])
        mean = sb("mean", [P, 2, TS])
        var = sb("var", [P, 2, TS])
        guard = sb("guard", [P, BUFS, TD + TE])
        sd = sb("sd", [P, 2 * TE])
        rs = sb("rs", [P, 2, 2 * TE])
        scs = sb("scs", [P, 2, TE])
        norms = sb("norms", [P, TE])
        bia = sb("bia", [P, 2, 2 * TE])
        ss = sb("ss", [P, BUFS, TD + TE])
        d2 = sb("d2", [P, TD + TE])
        dd = sb("dd", [P, TD + TE])
        rd = sb("rd", [P, TD + TE])
        junk = sb("junk", [P, TD + TE, D], BF16)
        idx = sb("idx", [P, STEPS, 4, 2, 2], I32)
        idl = sb("idl", [P, Q, 2], I32)
        lohi = sb("lohi", [P, 2, Q, 2])
        nd = sb("nd", [P, Q, 2])
        stage = sb("stage", [P, XBUFS, 3 * TE], I32)
        sstage = sb("sstage", [P, BUFS, TE], I32)
        lstage = sb("lstage", [P, 2, 2], I32)
        df = sb("df", [Q, QW])
        nf = sb("nf", [Q, QW])
        nl = sb("nl", [Q, QW])
        nf16 = sb("nf16", [Q, QW], BF16)
        cloc = sb("cloc", [Q, QW])
        fsm = sb("fsm", [Q, QW])
        onesq = sb("onesq", [Q, QW])
        iotai = sb("iotai", [P, J], I32)
        iotaf = sb("iotaf", [P, J], F16)
        ioq = sb("ioq", [Q, QW])
        rowi = sb("rowi", [Q, 2], I32)
        lim = sb("lim", [Q, 1])
        endc = sb("endc", [Q, 7])
        rows = sb("rows", [1, 9, P])
        flf = sb("flf", [Q, QW])
        flr = sb("flr", [Q, 1])
        fli = sb("fli", [1, 1], I32)
        lrow = sb("lrow", [P, 2, 2 * D])
        nat = xo[0:Q, 1, 0:5 * QW].bitcast(I32).rearrange("q (a w) -> q a w", a=5)
        natf = xo[0:Q, 0, :].rearrange("q (a w) -> q a w", a=8)
        ohl = ybuf[:, 0, 0:BUFS * P // 2].bitcast(F16).rearrange("p (b j) -> p b j", b=BUFS)
        ohh = ybuf[:, 1, 0:BUFS * J // 2].bitcast(F16).rearrange("p (b j) -> p b j", b=BUFS)
        tabs = xin[:, 0, 0:J]
        tabq = xin[:, 1, 0:J]
        ndq = xin[:, 2, 0:2 * Q]

        pt = ctx.enter_context(nc.psum_tensor("pt", [P, 2, 512], F32))
        pu = ctx.enter_context(nc.psum_tensor("pu", [P, 2, 512], F32))
        pe_s = ctx.enter_context(nc.psum_tensor("pe_s", [P, 512], F32))
        pe_d = ctx.enter_context(nc.psum_tensor("pe_d", [P, 512], F32))
        pe_m = ctx.enter_context(nc.psum_tensor("pe_m", [P, 512], F32))
        pe_x = ctx.enter_context(nc.psum_tensor("pe_x", [P, 512], F32))
        turned = [pt[:, 0, :], pt[:, 1, :], pu[:, 0, :], pu[:, 1, :], pe_s[:], pe_d[:], pe_m[:], pe_x[:]]

        s_filled = sem("s_filled")
        s_nat = sem("s_nat")
        s_w = sem("s_w")
        s_zero = sem("s_zero")
        s_ident = sem("s_ident")
        s_iota = sem("s_iota")
        s_const = sem("s_const")
        s_ch = sem("s_ch")
        s_endc = sem("s_endc")
        s_carryrow = sem("s_carryrow")
        s_late = sem("s_late")
        s_ends = sem("s_ends")
        s_carry = sem("s_carry")
        s_firstc = sem("s_firstc")
        s_firsts = sem("s_firsts")
        s_totalrow = sem("s_totalrow")
        s_totals = sem("s_totals")
        s_natf = sem("s_natf")
        s_turn = sem("s_turn")
        s_idx = sem("s_idx")
        s_cnt = sem("s_cnt")
        s_ndq = sem("s_ndq")
        s_oh = sem("s_oh")
        s_ohu = sem("s_ohu")
        s_tab = sem("s_tab")
        s_tabq = sem("s_tabq")
        s_tabr = sem("s_tabr")
        s_ntab = sem("s_ntab")
        s_nfd = sem("s_nfd")
        s_flag = sem("s_flag")
        s_setup = sem("s_setup")
        x_loaded = sems("x_loaded")
        same_loaded = sems("same_loaded")
        xs_got = sems("xs_got", XBUFS)
        xd_got = sems("xd_got", XBUFS)
        nsrc_got = sems("nsrc_got", XBUFS)
        out_stored = sems("out_stored")
        late_stored = sems("late_stored")
        scattered = sems("scattered")
        staged = sem("staged")
        sstaged = sem("sstaged")
        bn_done = sem("bn_done")
        st_chain = sem("st_chain")
        mean_ready = sem("mean_ready")
        var_ready = sem("var_ready")
        sd_ready = sem("sd_ready")
        rs_chain = sem("rs_chain")
        affine_ready = sem("affine_ready")
        relu_done = sem("relu_done")
        et_done = sem("et_done")
        hdt_done = sem("hdt_done")
        scan_done = sem("scan_done")
        prod_done = sem("prod_done")
        em_done = sem("em_done")
        msg_done = sem("msg_done")
        ye_done = sem("ye_done")
        t_done = sem("t_done")
        t_evac = sem("t_evac")
        m_done = sem("m_done")
        u_evac = sem("u_evac")
        y_done = sem("y_done")
        ss_done = sem("ss_done")
        d2_ready = sem("d2_ready")
        dd_ready = sem("dd_ready")
        rd_ready = sem("rd_ready")
        f_done = sem("f_done")
        late_got = sems("late_got", 2)
        late_put = sem("late_put")
        lstaged = sem("lstaged")

        def steps(eng, do, last):
            for i in range(UN):
                do(Step(0, i), i)
            with eng.Fori(1, LOOPS) as blk:
                for r in range(UN):
                    do(Step(blk, r), None)
            for i in range(LOOPS * UN, last + 1):
                do(Step(LOOPS, i - LOOPS * UN), i)

        def has(i, d):
            return i is None or 0 <= i + d < STEPS

        def chunk(t, s, i, d):
            if i is not None and i + d == STEPS - 1:
                return t[(STEPS - 1) * CH:N, :].rearrange("(p t) f -> p (t f)", t=TD), LASTP
            return t[bass.ds(s(d) * CH, CH), :].rearrange("(p t) f -> p (t f)", t=TD), P

        block = ctx.enter_context(nc.Block())

        @block.sync
        def _(sp):
            sp.dma_start(w1[:], W1).then_inc(s_w, 16)
            sp.dma_start(w2[:], W2).then_inc(s_w, 16)
            sp.wait_ge(s_filled, 1)
            flat = lambda t, a, b, q: t[a:b].rearrange("(q w) -> q w", q=q)
            sp.dma_start(nat[0:QF, 0, :], flat(dst, 0, QF * QW, QF)).then_inc(s_nat, 16)
            sp.dma_start(nat[QF:Q, 0, 0:QR], flat(dst, QF * QW, E, 1)).then_inc(s_nat, 16)
            sp.dma_start(nat[0:1, 1, 1:QW], flat(dst, 0, QW - 1, 1)).then_inc(s_nat, 16)
            sp.dma_start(nat[1:QF, 1, :], flat(dst, QW - 1, QF * QW - 1, QF - 1)).then_inc(s_nat, 16)
            sp.dma_start(nat[QF:Q, 1, 0:QR + 1], flat(dst, QF * QW - 1, E, 1)).then_inc(s_nat, 16)
            sp.dma_start(nat[0:QF, 2, :], flat(dst, 1, QF * QW + 1, QF)).then_inc(s_nat, 16)
            sp.dma_start(nat[QF:Q, 2, 0:QR - 1], flat(dst, QF * QW + 1, E, 1)).then_inc(s_nat, 16)
            sp.dma_start(nat[0:QF, 3, :], flat(src, 0, QF * QW, QF)).then_inc(s_nat, 16)
            sp.dma_start(nat[QF:Q, 3, 0:QR], flat(src, QF * QW, E, 1)).then_inc(s_nat, 16)
            sp.wait_ge(s_natf, 1)
            sp.dma_start(nfd, nf16[:]).then_inc(s_nfd, 16)
            sp.wait_ge(s_late, 1)
            sp.dma_start(flagd, fli[:]).then_inc(s_flag, 16)
            sp.wait_ge(s_tabr, 1)
            sp.dma_start(ntab.rearrange("(p j) o -> p (j o)", p=P), tabs).then_inc(s_ntab, 16)
            sp.wait_ge(s_nfd, 16)
            sp.wait_ge(s_ntab, 16)
            sp.wait_ge(s_setup, 1)
            same_flat = nfd.rearrange("q w -> (q w)")

            def do(s, i):
                if has(i, 0):
                    if has(i, -4):
                        sp.wait_ge(f_done, s(-3))
                    src_rows, np_ = chunk(x, s, i, 0)
                    sp.dma_start(xin[0:np_, s.buf(), :], src_rows).then_inc(x_loaded[s.buf()], 16)
                    sp.dma_start(
                        same[:, s.buf(), :],
                        same_flat[bass.ds(s() * (TE * P), TE * P)].rearrange("(o w) -> o w", o=1).to_broadcast([P, TE * P]),
                    ).then_inc(same_loaded[s.buf()], 16)
                if has(i, -4):
                    sp.wait_ge(f_done, s(-3))
                    dst_rows, np_ = chunk(out, s, i, -4)
                    sp.dma_start(dst_rows, xo[0:np_, s.buf(-4, 2), :]).then_inc(out_stored[s.buf(-4)], 16)
                    sp.dma_start(lated[bass.ds(s(-4) * (2 * P), 2 * P), :].rearrange("(h p) w -> p h w", h=2),
                                 oe[:, s.buf(-4), :, :].rearrange("p (h t) f -> p h (t f)", h=2)
                                 ).then_inc(late_stored[s.buf(-4)], 16)

            steps(sp, do, STEPS + 3)
            for b in range(BUFS):
                n = len(range(b, STEPS, BUFS))
                sp.wait_ge(out_stored[b], 16 * n)
                sp.wait_ge(late_stored[b], 16 * n)

        @block.gpsimd
        def _(pool):
            pool.memset(ident[:], 0.0).then_inc(s_zero, 1)
            pool.iota(iotai[:], pattern=[[1, J]], base=0, channel_multiplier=0)
            pool.iota(rowi[:, 0:1], pattern=[[0, 1]], base=0, channel_multiplier=1).then_inc(s_iota, 1)
            pool.wait_ge(s_zero, 1)
            pool.affine_select(out=ident[:], in_=ident[:], compare_op=ALU.not_equal, fill=1.0, base=0,
                               pattern=[[-1, P]], channel_multiplier=1).then_inc(s_ident, 1)
            pool.wait_ge(s_idx, 1)
            row_limit = pool.to_reg(N - 1)
            tab_limit = pool.to_reg(P * J - 1)

            def gather(to, rows, index, limit, done):
                pool.indirect_dma_start(out=to, out_offset=None, in_=rows,
                                        in_offset=bass.IndirectOffsetOnAxis(ap=index, axis=0),
                                        bounds_check=limit, oob_is_err=False).then_inc(done, 16)

            def scatter(rows, index, done):
                pool.indirect_dma_start(out=out, out_offset=bass.IndirectOffsetOnAxis(ap=index, axis=0),
                                        in_=rows, in_offset=None,
                                        bounds_check=row_limit, oob_is_err=False).then_inc(done, 16)

            def stage_gather(s, d):
                pool.tensor_copy(stage[:, s.buf(d, XBUFS), :],
                                 idx[:, bass.ds(s(d), 1), 0:3, :, :].rearrange("p o a q h -> p (o a q h)")
                                 ).then_inc(staged, 1)

            def stage_scatter(s, d):
                pool.tensor_copy(sstage[:, s.buf(d), :],
                                 idx[:, bass.ds(s(d), 1), 3:4, :, :].rearrange("p o a q h -> p (o a q h)")
                                 ).then_inc(sstaged, 1)

            def gather_rows(s, i, d):
                b = s.buf(d, XBUFS)
                pool.wait_ge(staged, s(d + 1))
                if has(i, d + 1):
                    stage_gather(s, d + 1)
                for k in range(TE):
                    gather(xs[:, b, k, :], x, stage[:, b, k:k + 1], row_limit, xs_got[b])
                for k in range(TE):
                    gather(xd[:, b, k, :], x, stage[:, b, TE + k:TE + k + 1], row_limit, xd_got[b])

            stage_gather(Step(0, 0), 0)
            stage_scatter(Step(0, 0), 0)
            for i in range(4):
                gather_rows(Step(0, i), i, 0)
            pool.wait_ge(s_ntab, 16)

            def do(s, i):
                if has(i, 4):
                    if has(i, -4):
                        pool.wait_ge(relu_done, s(-3))
                        pool.wait_ge(f_done, s(-3))
                    if has(i, -3):
                        b = s.buf(-3, XBUFS)
                        pool.wait_ge(xs_got[b], s.dma(-3, TE, XBUFS))
                        pool.wait_ge(xd_got[b], s.dma(-3, TE, XBUFS))
                        pool.wait_ge(nsrc_got[b], s.dma(-3, TE, XBUFS))
                    gather_rows(s, i, 4)
                if has(i, 0):
                    b = s.buf(0, XBUFS)
                    for k in range(TE):
                        gather(nsrc[:, b, k:k + 1], ntab, stage[:, b, 2 * TE + k:2 * TE + k + 1], tab_limit,
                               nsrc_got[b])
                if has(i, -4):
                    b = s.buf(-4)
                    pool.wait_ge(f_done, s(-3))
                    pool.wait_ge(out_stored[b], s.dma(-4))
                    if has(i, -5):
                        pool.wait_ge(out_stored[s.buf(-5)], s.dma(-5))
                    if has(i, -7):
                        pool.wait_ge(scattered[s.buf(-7)], s.dma(-7, TE))
                    pool.wait_ge(sstaged, s(-3))
                    if has(i, -3):
                        stage_scatter(s, -3)
                    for k in range(TE):
                        scatter(oe[:, b, k, :], sstage[:, b, k:k + 1], scattered[b])

            steps(pool, do, STEPS + 3)
            for b in range(BUFS):
                n = len(range(b, STEPS, BUFS))
                pool.wait_ge(scattered[b], 16 * TE * n)
                pool.wait_ge(out_stored[b], 16 * n)
                pool.wait_ge(late_stored[b], 16 * n)
            pool.wait_ge(s_flag, 16)
            late = pool.value_load(flagd, min_val=0, max_val=1)
            with pool.If(late > 0):
                def bring(q, b):
                    pool.tensor_copy(lstage[:, b, :], idl[:, bass.ds(q, 1), :].rearrange("p o h -> p (o h)")
                                     ).then_inc(lstaged, 1)
                    pool.dma_start(lrow[:, b, :], lated[bass.ds(q * P, P), :]).then_inc(late_got[b], 16)

                def put(q, b, times, first=False, last=False):
                    pool.wait_ge(late_got[b], times * 16 + 16)
                    if not first:
                        pool.wait_ge(late_put, q * 32)
                    pool.wait_ge(lstaged, q + 1)
                    if not last:
                        bring(q + 1, 1 - b)
                    for h in range(2):
                        scatter(lrow[:, b, h * D:(h + 1) * D], lstage[:, b, h:h + 1], late_put)

                bring(0, 0)
                put(0, 0, 0, first=True)
                with pool.Fori(0, Q // 2 - 1) as half:
                    put(half * 2 + 1, 1, half)
                    put(half * 2 + 2, 0, half + 1)
                put(Q - 1, 1, Q // 2 - 1, last=True)
                pool.wait_ge(late_put, 32 * Q)
            pool.nop()

        @block.vector
        def _(dve):
            link = [0]

            def chain(ins):
                link[0] += 1
                ins.then_inc(s_ch, 1)
                dve.wait_ge(s_ch, link[0])

            dve.memset(nat[:, 0, :], int(PAD))
            dve.memset(nat[:, 1:3, :], -1)
            dve.memset(nat[:, 3, :], 0).then_inc(s_filled, 1)
            dve.memset(eps[:], EPS)
            dve.memset(zero[:], 0.0)
            dve.memset(ones[:], 1.0)
            dve.memset(rows[:], 0.0)
            dve.memset(onesq[:], 1.0)
            dve.memset(guard[:], NORM_MIN * NORM_MIN)
            dve.wait_ge(s_iota, 1)
            dve.tensor_copy(iotaf[:], iotai[:])
            dve.tensor_scalar(ioq[:], iotai[0:Q, 0:QW], 1.0, None, ALU.add)
            chain(dve.tensor_scalar(rowi[:, 1:2], rowi[:, 0:1], 1, None, ALU.logical_shift_right))
            dve.tensor_scalar(lim[:], rowi[:, 1:2], float(CH), float(CH - 1), ALU.mult, ALU.add)
            dve.wait_ge(s_ident, 1)
            dve.tensor_scalar(nident[:], ident[:], -1.0, None, ALU.mult).then_inc(s_const, 1)
            dve.wait_ge(s_nat, 16 * 9)
            chain(dve.tensor_scalar(nat[:, 4, :], nat[:, 0, :], P - 1, None, ALU.bitwise_and))
            chain(dve.tensor_copy(natf[:, 5, :], nat[:, 4, :]))
            chain(dve.tensor_scalar(nat[:, 4, :], nat[:, 0, :], 7, None, ALU.logical_shift_right))
            chain(dve.tensor_copy(natf[:, 6, :], nat[:, 4, :]))
            chain(dve.tensor_scalar(nat[:, 4, :], nat[:, 3, :], P - 1, None, ALU.bitwise_and))
            dve.tensor_copy(natf[:, 0, :], nat[:, 3, :])
            chain(dve.tensor_copy(cloc[:], nat[:, 4, :]))
            chain(dve.tensor_scalar(nat[:, 4, :], nat[:, 3, :], 7, None, ALU.logical_shift_right))
            chain(dve.tensor_copy(fsm[:], nat[:, 4, :]))
            dve.scalar_tensor_tensor(natf[:, 2, :], cloc[:], float(J), fsm[:], ALU.mult, ALU.add)
            chain(dve.tensor_copy(df[:], nat[:, 0, :]))
            dve.tensor_scalar(natf[:, 1, :], df[:], float(N - 1), None, ALU.min)
            chain(dve.tensor_tensor(nf[:], nat[:, 0, :], nat[:, 1, :], ALU.is_equal))
            dve.tensor_tensor(nl[:], nat[:, 0, :], nat[:, 2, :], ALU.is_equal)
            dve.tensor_copy(nf16[:], nf[:])
            chain(dve.tensor_tensor_scan(cloc[:], nf[:], onesq[:], 0.0, ALU.mult, ALU.add))
            dve.tensor_copy(endc[:, 0:1], cloc[:, QW - 1:QW])
            dve.tensor_copy(endc[:, 2:3], nf[:, 0:1])
            dve.scalar_tensor_tensor(endc[:, 1:2], cloc[:, QW - 1:QW], float(QW), nf[:, 0:1],
                                     ALU.is_equal, ALU.mult)
            chain(dve.tensor_tensor(fsm[:], cloc[:], ioq[:], ALU.is_equal))
            chain(dve.tensor_scalar(flf[:], df[:], lim[:, 0:1], None, ALU.is_gt))
            chain(dve.tensor_tensor(natf[:, 7, :], flf[:], nl[:], ALU.max))
            chain(dve.scalar_tensor_tensor(natf[:, 3, :], natf[:, 7, :], PAD, df[:], ALU.mult, ALU.add))
            chain(dve.tensor_scalar(natf[:, 7, :], flf[:], -1.0, 1.0, ALU.mult, ALU.add))
            chain(dve.tensor_tensor(flf[:], natf[:, 7, :], nl[:], ALU.max))
            chain(dve.scalar_tensor_tensor(natf[:, 4, :], flf[:], PAD, df[:], ALU.mult, ALU.add))
            chain(dve.tensor_scalar(flf[:], natf[:, 4, :], float(N), None, ALU.is_lt))
            chain(dve.tensor_reduce(endc[:, 4:5], flf[:], AX.X, ALU.max))
            dve.tensor_copy(endc[:, 3:4], endc[:, 0:1]).then_inc(s_endc, 1)
            dve.wait_ge(s_ends, 1)
            for k in range(3):
                dve.tensor_copy(rows[0:1, k, 0:Q], pe_s[0:1, k * P:k * P + Q])
            chain(dve.tensor_reduce(rows[0:1, 5, 0:1], pe_s[0:1, 3 * P:3 * P + Q], AX.X, ALU.max))
            dve.tensor_copy(fli[:], rows[0:1, 5, 0:1]).then_inc(s_late, 1)
            chain(dve.tensor_tensor_scan(rows[0:1, 3, 0:Q], rows[0:1, 1, 0:Q], rows[0:1, 0, 0:Q], 0.0,
                                         ALU.mult, ALU.add))
            dve.tensor_tensor(rows[0:1, 4, 1:Q], rows[0:1, 2, 1:Q], rows[0:1, 3, 0:Q - 1], ALU.mult).then_inc(s_carryrow, 1)
            dve.wait_ge(s_carry, 1)
            chain(dve.tensor_copy(flr[:], pe_d[0:Q, 0:1]))
            chain(dve.scalar_tensor_tensor(natf[:, 7, :], fsm[:], flr[:, 0:1], cloc[:], ALU.mult, ALU.add))
            chain(dve.tensor_scalar(fsm[:], nl[:], -1.0, 1.0, ALU.mult, ALU.add))
            chain(dve.tensor_tensor(flf[:], fsm[:], natf[:, 7, :], ALU.mult))
            chain(dve.tensor_tensor_scan(cloc[:, ::-1], nl[:, ::-1], flf[:, ::-1], 0.0, ALU.mult, ALU.add))
            dve.tensor_copy(endc[:, 5:6], cloc[:, 0:1])
            dve.tensor_scalar(endc[:, 6:7], cloc[:, 0:1], 0.0, None, ALU.is_equal).then_inc(s_firstc, 1)
            chain(dve.tensor_scalar(fsm[:], cloc[:], 0.0, None, ALU.is_equal))
            dve.wait_ge(s_firsts, 1)
            for k in range(2):
                last = dve.tensor_copy(rows[0:1, 6 + k, 0:Q], pe_s[0:1, k * P:k * P + Q])
            chain(last)
            dve.tensor_tensor_scan(rows[0:1, 8, Q - 1::-1], rows[0:1, 7, Q - 1::-1], rows[0:1, 6, Q - 1::-1], 0.0,
                                   ALU.mult, ALU.add).then_inc(s_totalrow, 1)
            dve.wait_ge(s_totals, 1)
            chain(dve.tensor_copy(flr[:], pe_d[0:Q, 0:1]))
            dve.scalar_tensor_tensor(natf[:, 7, :], fsm[:], flr[:, 0:1], cloc[:], ALU.mult, ALU.add
                                     ).then_inc(s_natf, 1)
            dve.wait_ge(s_turn, 1)
            for h in range(2):
                for a in range(8):
                    col = turned[a][:, h * P:h * P + Q]
                    if a < 4:
                        dve.tensor_copy(idx[:, :, a, :, h], col.rearrange("p (b q) -> p b q", q=2))
                    elif a == 4:
                        dve.tensor_copy(idl[:, :, h], col)
                    elif a < 7:
                        dve.tensor_copy(lohi[:, a - 5, :, h], col)
                    else:
                        last = dve.tensor_copy(nd[:, :, h], col)
            last.then_inc(s_idx, 1)
            dve.wait_ge(s_idx, 1)
            dve.wait_ge(s_ndq, 1)
            dve.reciprocal(nd[:].rearrange("p q h -> p (q h)"), ndq)
            col = lohi[:].rearrange("p a q h -> p a (q h)")

            def onehot(g, k, wait):
                if wait:
                    dve.wait_ge(s_ohu, g - (BUFS - 1))
                dve.tensor_scalar(ohl[:, k, :], iotaf[:, 0:P], col[:, 0, bass.ds(g, 1)], None, ALU.is_equal)
                dve.tensor_scalar(ohh[:, k, :], iotaf[:], col[:, 1, bass.ds(g, 1)], None, ALU.is_equal
                                  ).then_inc(s_oh, 1)

            for k in range(BUFS):
                onehot(k, k, False)
            with dve.Fori(1, G // BUFS) as b:
                for k in range(BUFS):
                    onehot(b * BUFS + k, k, True)
            dve.wait_ge(s_ohu, G)
            dve.tensor_scalar(tabs[:, 0:512], pt[:, 0, :], 1.0, None, ALU.max)
            dve.tensor_scalar(tabs[:, 512:J], pt[:, 1, 0:J - 512], 1.0, None, ALU.max).then_inc(s_tab, 1)
            dve.wait_ge(s_tabq, 1)
            dve.reciprocal(tabs, tabq).then_inc(s_tabr, 1)
            dve.wait_ge(s_tabr, 1)
            dve.memset(zero[:], 0.0).then_inc(s_setup, 1)

            def statistics(s, d):
                b, e, h = s.buf(d), s.buf(d, XBUFS), s.buf(d, 2)
                dve.wait_ge(x_loaded[b], s.dma(d))
                for t in range(TD):
                    dve.bn_stats(bst[:, t, :], xin[:, b, t * D:(t + 1) * D])
                dve.wait_ge(xs_got[e], s.dma(d, TE, XBUFS))
                for t in range(TE):
                    dve.bn_stats(bst[:, TD + t, :], xs[:, e, t, :])
                dve.wait_ge(xd_got[e], s.dma(d, TE, XBUFS))
                for t in range(TE):
                    last = dve.bn_stats(bst[:, TD + TE + t, :], xd[:, e, t, :])
                last.then_inc(bn_done, 1)
                dve.wait_ge(bn_done, s(d + 1))
                dve.tensor_tensor(msum[:], bst[:, :, 1], bst[:, :, 4], ALU.add)
                dve.tensor_tensor(mdif[:], bst[:, :, 1], bst[:, :, 4], ALU.subtract)
                dve.tensor_tensor(m2[:], bst[:, :, 2], bst[:, :, 5], ALU.add).then_inc(st_chain, 1)
                dve.wait_ge(st_chain, s(d) * 2 + 1)
                dve.tensor_scalar(mean[:, h, :], msum[:], 0.5, None, ALU.mult).then_inc(mean_ready, 1)
                dve.scalar_tensor_tensor(dsq[:], mdif[:], 0.25, mdif[:], ALU.mult, ALU.mult).then_inc(st_chain, 1)
                dve.wait_ge(st_chain, s(d) * 2 + 2)
                dve.scalar_tensor_tensor(var[:, h, :], m2[:], 1.0 / D, dsq[:], ALU.mult, ALU.add
                                         ).then_inc(var_ready, 1)
                dve.wait_ge(var_ready, s(d + 1))
                dve.tensor_scalar(guard[:, b, 0:TD], var[:, h, 0:TD], EPS, NORM_MIN * NORM_MIN, ALU.add, ALU.mult)

            ndf = nd[:].rearrange("p q h -> p (q h)")
            statistics(Step(0, 0), 0)

            def do(s, i):
                if has(i, -1):
                    b, h, hp = s.buf(-1), s.buf(-1, 2), s.buf(-2, 2)
                    dve.wait_ge(et_done, s())
                    dve.wait_ge(same_loaded[b], s.dma(-1))
                    if has(i, -3):
                        dve.wait_ge(em_done, s(-2))
                    if i == 1:
                        start = 0.0
                    else:
                        dve.wait_ge(scan_done, s(-1))
                        start = agg[:, hp, TE * P - 1:TE * P]
                    dve.tensor_tensor_scan(agg[:, h, :], same[:, b, :], pe_s[:], start, ALU.mult, ALU.add
                                           ).then_inc(scan_done, 1)
                    dve.wait_ge(scan_done, s())
                    dve.wait_ge(hdt_done, s())
                    dve.tensor_tensor(prod[:, h, :], agg[:, h, :], hdt[:, h, :], ALU.mult).then_inc(prod_done, 1)
                if has(i, 0):
                    e, h = s.buf(0, XBUFS), s.buf(0, 2)
                    dve.wait_ge(sd_ready, s(1))
                    if has(i, -2):
                        dve.wait_ge(relu_done, s(-1))
                    dve.reciprocal(rs[:, h, :], sd[:]).then_inc(rs_chain, 1)
                    dve.wait_ge(nsrc_got[e], s.dma(0, TE, XBUFS))
                    dve.tensor_tensor(norms[:], nsrc[:, e, :], ndf[:, bass.ds(s() * TE, TE)], ALU.mult
                                      ).then_inc(rs_chain, 1)
                    dve.wait_ge(rs_chain, s() * 3 + 2)
                    dve.scalar_tensor_tensor(bia[:, h, TE:2 * TE], mean[:, h, TD + TE:TS], -1.0, rs[:, h, TE:2 * TE],
                                             ALU.mult, ALU.mult)
                    dve.tensor_tensor(scs[:, h, :], rs[:, h, 0:TE], norms[:], ALU.mult).then_inc(rs_chain, 1)
                    dve.wait_ge(rs_chain, s() * 3 + 3)
                    dve.scalar_tensor_tensor(bia[:, h, 0:TE], mean[:, h, TD:TD + TE], -1.0, scs[:, h, :],
                                             ALU.mult, ALU.mult).then_inc(affine_ready, 1)
                if has(i, -1):
                    yb = ybuf[:, s.buf(-1), :]
                    dve.wait_ge(u_evac, s() * NQ)
                    dve.scalar_tensor_tensor(yb, yb, SLOPE, yb, ALU.mult, ALU.max).then_inc(y_done, 1)
                if has(i, -2):
                    dve.wait_ge(ss_done, s(-1))
                    dve.tensor_tensor(d2[:], ss[:, s.buf(-2), :], guard[:, s.buf(-2), :], ALU.max).then_inc(d2_ready, 1)
                if has(i, 1):
                    statistics(s, 1)
                if has(i, -2):
                    b, e = s.buf(-2), s.buf(-2, XBUFS)
                    dve.wait_ge(dd_ready, s(-1))
                    dve.reciprocal(rd[:], dd[:]).then_inc(rd_ready, 1)
                    dve.wait_ge(rd_ready, s(-1))
                    if has(i, -6):
                        dve.wait_ge(scattered[b], s.dma(-6, TE))
                        dve.wait_ge(late_stored[b], s.dma(-6))
                    for t in range(TE):
                        dve.scalar_tensor_tensor(oe[:, b, t, :], ye[:, b, t * D:(t + 1) * D], rd[:, TD + t:TD + t + 1],
                                                 xd[:, e, t, :], ALU.mult, ALU.add)
                    if has(i, -4):
                        dve.wait_ge(out_stored[s.buf(-4)], s.dma(-4))
                    for t in range(TD):
                        f = slice(t * D, (t + 1) * D)
                        last = dve.scalar_tensor_tensor(xo[:, s.buf(-2, 2), f], ybuf[:, b, f], rd[:, t:t + 1],
                                                        xin[:, b, f], ALU.mult, ALU.add)
                    last.then_inc(f_done, 1)
                if has(i, -1):
                    mb = msg[:, s.buf(-1, 2), :]
                    dve.wait_ge(msg_done, s())
                    dve.scalar_tensor_tensor(ye[:, s.buf(-1), :], mb, SLOPE, mb, ALU.mult, ALU.max
                                             ).then_inc(ye_done, 1)

            steps(dve, do, STEPS + 1)

        @block.scalar
        def _(act):
            act.wait_ge(s_idx, 1)
            act.activation(ndq, nd[:].rearrange("p q h -> p (q h)"), ACT.Sqrt).then_inc(s_ndq, 1)
            act.wait_ge(s_tab, 1)
            act.activation(tabq, tabs, ACT.Sqrt).then_inc(s_tabq, 1)

            def do(s, i):
                def relu_quarter(q):
                    act.wait_ge(t_done, s() * NQ + (q + 1))
                    if q >= 2 or has(i, -1):
                        act.wait_ge(m_done, s() * NQ + (q - 1))
                    act.activation(ct[:, q % 2, :], pt[:, q % 2, :], ACT.Relu).then_inc(t_evac, 1)

                def copy_quarter(q):
                    act.wait_ge(m_done, s() * NQ + (q + 1))
                    act.copy(ybuf[:, s.buf(), q * 512:(q + 1) * 512], pu[:, q % 2, :]).then_inc(u_evac, 1)

                def relu_rows(to, rows, scale, bias):
                    for t in range(TE):
                        last = act.activation(to[:, t, :], rows[:, t, :], ACT.Relu, bias=bias[:, t:t + 1],
                                              scale=scale[:, t:t + 1])
                    return last

                def squares(first, last):
                    b = s.buf(-1)
                    for t in range(first, last):
                        act.activation(junk[:, t, :], ybuf[:, b, t * D:(t + 1) * D], ACT.Square,
                                       accum_out=ss[:, b, t:t + 1])

                if has(i, 0):
                    act.wait_ge(var_ready, s(1))
                    if has(i, -1):
                        act.wait_ge(affine_ready, s())
                    act.activation(sd[:], var[:, s.buf(0, 2), TD:TS], ACT.Sqrt, bias=eps[:, 0:1]).then_inc(sd_ready, 1)
                if has(i, -1):
                    act.wait_ge(et_done, s())
                    if has(i, -3):
                        act.wait_ge(em_done, s(-2))
                        act.wait_ge(prod_done, s(-2))
                    act.copy(hdt[:, s.buf(-1, 2), :], pe_d[:]).then_inc(hdt_done, 1)
                if has(i, 0):
                    relu_quarter(0)
                    relu_quarter(1)
                    if has(i, -4):
                        act.wait_ge(f_done, s(-3))
                    copy_quarter(0)
                if has(i, -2):
                    b = s.buf(-2)
                    act.wait_ge(ye_done, s(-1))
                    for t in range(TE):
                        last = act.activation(junk[:, TD + t, :], ye[:, b, t * D:(t + 1) * D], ACT.Square,
                                              accum_out=ss[:, b, TD + t:TD + t + 1])
                    last.then_inc(ss_done, 1)
                if has(i, 0):
                    e, h = s.buf(0, XBUFS), s.buf(0, 2)
                    act.wait_ge(affine_ready, s(1))
                    if has(i, -2):
                        act.wait_ge(et_done, s(-1))
                    relu_rows(hs[:, h], xs[:, e], scs[:, h], bia[:, h, 0:TE])
                    relu_quarter(2)
                    copy_quarter(1)
                if has(i, -2):
                    act.wait_ge(d2_ready, s(-1))
                    if has(i, -3):
                        act.wait_ge(rd_ready, s(-2))
                    act.activation(dd[:], d2[:], ACT.Sqrt).then_inc(dd_ready, 1)
                if has(i, 0):
                    relu_rows(hd[:, h], xd[:, e], rs[:, h, TE:2 * TE], bia[:, h, TE:2 * TE]).then_inc(relu_done, 1)
                    relu_quarter(3)
                    copy_quarter(2)
                if has(i, -1):
                    act.wait_ge(y_done, s())
                    squares(0, 4)
                    act.wait_ge(em_done, s())
                    if has(i, -3):
                        act.wait_ge(ye_done, s(-2))
                    act.copy(msg[:, s.buf(-1, 2), :], pe_m[:]).then_inc(msg_done, 1)
                if has(i, 0):
                    copy_quarter(3)
                if has(i, -1):
                    squares(4, TD)

            steps(act, do, STEPS + 1)

        @block.tensor
        def _(pe):
            pe.wait_ge(s_const, 1)
            pe.wait_ge(s_endc, 1)
            for k, c in enumerate((0, 1, 2, 4)):
                last = pe.matmul(pe_s[0:1, k * P:k * P + Q], endc[:, c:c + 1], ident[0:Q, 0:Q], start=True, stop=True)
            last.then_inc(s_ends, 1)
            pe.wait_ge(s_carryrow, 1)
            pe.matmul(pe_d[0:Q, 0:1], rows[0:1, 4, 0:Q], ones[0:1, 0:1], start=True, stop=True).then_inc(s_carry, 1)
            pe.wait_ge(s_firstc, 1)
            for k in range(2):
                last = pe.matmul(pe_s[0:1, k * P:k * P + Q], endc[:, 5 + k:6 + k], ident[0:Q, 0:Q], start=True, stop=True)
            last.then_inc(s_firsts, 1)
            pe.wait_ge(s_totalrow, 1)
            pe.matmul(pe_d[0:Q, 0:1], rows[0:1, 8, 1:Q + 1], ones[0:1, 0:1], start=True, stop=True).then_inc(s_totals, 1)
            pe.wait_ge(s_natf, 1)
            for a in range(8):
                for h in range(2):
                    last = pe.transpose(turned[a][:, h * P:h * P + Q], natf[:, a, h * P:(h + 1) * P], ident[0:Q, 0:Q])
            last.then_inc(s_turn, 1)
            pe.wait_ge(s_idx, 1)

            def count(g, k, first, final):
                pe.wait_ge(s_oh, g + 1)
                pe.matmul(pt[:, 0, :], ohl[:, k, :], ohh[:, k, 0:512], start=first, stop=final)
                pe.matmul(pt[:, 1, 0:J - 512], ohl[:, k, :], ohh[:, k, 512:J], start=first, stop=final
                          ).then_inc(s_ohu, 1)

            for k in range(BUFS):
                count(k, k, k == 0, False)
            with pe.Fori(1, G // BUFS - 1) as b:
                for k in range(BUFS):
                    count(b * BUFS + k, k, False, False)
            for k in range(BUFS):
                count(G - BUFS + k, k, False, k == BUFS - 1)
            pe.wait_ge(s_tab, 1)
            pe.wait_ge(s_w, 32)

            def do(s, i):
                def turn_quarter(q):
                    if q >= 2 or has(i, -1):
                        pe.wait_ge(t_evac, s() * NQ + (q - 1))
                    for t in range(4):
                        f = slice(t * D, (t + 1) * D)
                        col = q * 4 + t
                        pe.matmul(pt[:, q % 2, f], xin[:, s.buf(), col * D:(col + 1) * D], ident[:],
                                  is_transpose=True, start=True, stop=False)
                        last = pe.matmul(pt[:, q % 2, f], mean[:, s.buf(0, 2), col:col + 1].to_broadcast([P, D]),
                                         nident[:], start=False, stop=True)
                    last.then_inc(t_done, 1)

                def mul_quarter(q):
                    pe.wait_ge(t_evac, s() * NQ + (q + 1))
                    if q >= 2 or has(i, -1):
                        pe.wait_ge(u_evac, s() * NQ + (q - 1))
                    for t in range(4):
                        f = slice(t * D, (t + 1) * D)
                        last = pe.matmul(pu[:, q % 2, f], ct[:, q % 2, f], w1[:], start=True, stop=True)
                    last.then_inc(m_done, 1)

                if has(i, 0):
                    pe.wait_ge(mean_ready, s(1))
                    turn_quarter(0)
                    turn_quarter(1)
                    mul_quarter(0)
                    turn_quarter(2)
                    mul_quarter(1)
                    turn_quarter(3)
                if has(i, -1):
                    h = s.buf(-1, 2)
                    pe.wait_ge(hdt_done, s())
                    pe.wait_ge(prod_done, s())
                    if has(i, -2):
                        pe.wait_ge(msg_done, s(-1))
                    for t in range(TE):
                        f = slice(t * D, (t + 1) * D)
                        pe.matmul(pe_m[:, f], hdt[:, h, f], w1[:], start=True, stop=False)
                        pe.matmul(pe_m[:, f], agg[:, h, f], w1[:], start=False, stop=False)
                        last = pe.matmul(pe_m[:, f], prod[:, h, f], w2[:], start=False, stop=True)
                    last.then_inc(em_done, 1)
                if has(i, 0):
                    mul_quarter(2)
                    mul_quarter(3)
                    h = s.buf(0, 2)
                    pe.wait_ge(relu_done, s(1))
                    if has(i, -1):
                        pe.wait_ge(scan_done, s())
                        pe.wait_ge(hdt_done, s())
                    for t in range(TE):
                        f = slice(t * D, (t + 1) * D)
                        pe.transpose(pe_s[:, f], hs[:, h, t, :], ident[:])
                        last = pe.transpose(pe_d[:, f], hd[:, h, t, :], ident[:])
                    last.then_inc(et_done, 1)

            steps(pe, do, STEPS)


def kernel(**inputs):
    import concourse.bacc as bacc
    from concourse.bass_utils import run_bass_kernel_spmd

    nc = bacc.Bacc("TRN2", target_bir_lowering=False, num_devices=1)
    arrays, args = {}, []
    for name in ("x", "src", "dst", "L0_gnn_W1", "L0_gnn_W2"):
        a = np.ascontiguousarray(inputs[name])
        arrays[f"in_{name}"] = a
        args.append(nc.dram_tensor(f"in_{name}", a.shape, mybir.dt.from_np(a.dtype), kind="ExternalInput").ap())
    out = nc.dram_tensor("out", arrays["in_x"].shape, F32, kind="ExternalOutput").ap()
    gnn_preln_kernel(nc, *args, out)
    r = run_bass_kernel_spmd(nc, [arrays], core_ids=[0])
    return r.results[0]["out"]
```

```python
from contextlib import ExitStack

import numpy as np
import concourse.bass as bass
from concourse import mybir

ALU = mybir.AluOpType
ACT = mybir.ActivationFunctionType
AX = mybir.AxisListType
F32 = mybir.dt.float32
F16 = mybir.dt.float16
BF16 = mybir.dt.bfloat16
I32 = mybir.dt.int32

P = 128
D = 128
EPS = 1e-5
NORM_MIN = 1e-12
SLOPE = 0.2

TD = 16
TE = 4
TS = TD + 2 * TE
NQ = TD // 4
BUFS = 4
XBUFS = 12
UN = 12


class Step:

    def __init__(self, blk, r):
        self.blk, self.r = blk, r

    def __call__(self, d=0):
        return self.blk * UN + (self.r + d)

    def buf(self, d=0, n=BUFS):
        return (self.r + d) % n

    def dma(self, d=0, per=1, n=BUFS):
        return (self.blk * (UN // n) + ((self.r + d) // n + 1)) * (16 * per)


def gnn_preln_kernel(nc, x, src, dst, W1, W2, out):
    N = x.shape[0]
    E = src.shape[0]
    CH = P * TD
    STEPS = -(-N // CH)
    G = STEPS * TE
    assert G * P >= E and D == x.shape[1]
    LASTP = (N - (STEPS - 1) * CH) // TD
    assert (STEPS - 1) * CH + LASTP * TD == N
    Q = G // 2
    QW = 2 * P
    QF = E // QW
    QR = E - QF * QW
    assert QF == Q - 1 and 0 < QR < QW
    LO = 2 * P
    J = -(-N // LO)
    HU = 12
    assert (G - BUFS) % HU == 0
    TURNS = (G - BUFS) // HU
    PAD = float(1 << 20)
    EARLY = XBUFS - 3
    SKIPS = (4, 8)
    AHEAD = EARLY - len(SKIPS)
    NORMS = 3
    LOOPS = (STEPS - 1 - AHEAD) // UN

    ntab = nc.dram_tensor("norm_table", [LO * J, 1], F32).ap()
    nfd = nc.dram_tensor("same_segment", [Q, QW], BF16).ap()
    unsortd = nc.dram_tensor("unsorted_rows", [Q, 1], F32).ap()
    GP = G * P
    CW = 4 * P
    padded = nc.dram_tensor("padded_edges", [2, GP], I32).ap()
    sdst = nc.dram_tensor("sorted_dst", [GP + 2, 1], I32).ap()
    ssrc = nc.dram_tensor("sorted_src", [GP + 2, 1], I32).ap()
    flagd = nc.dram_tensor("late_flag", [1, 1], I32).ap()
    lated = nc.dram_tensor("edge_rows", [Q * P, 2 * D], F32).ap()

    with ExitStack() as ctx:
        def sb(name, shape, dt=F32):
            return ctx.enter_context(nc.sbuf_tensor(name, shape, dt))

        def sem(name):
            return ctx.enter_context(nc.semaphore(name))

        def sems(name, n=BUFS):
            return [sem(f"{name}{i}") for i in range(n)]

        ident = sb("ident", [P, P])
        nident = sb("nident", [P, P])
        w1 = sb("w1", [P, D])
        w2 = sb("w2", [P, D])
        eps = sb("eps", [P, 1])
        ones = sb("ones", [1, 1])
        xin = sb("xin", [P, BUFS, TD * D])
        ybuf = sb("ybuf", [P, BUFS, TD * D])
        xo = sb("xo", [P, 2, TD * D])
        ct = sb("ct", [P, 2, 4 * D])
        xs = sb("xs", [P, XBUFS, TE, D])
        xd = sb("xd", [P, XBUFS, TE, D])
        nsrc = sb("nsrc", [P, XBUFS, TE])
        same = sb("same", [P, BUFS, TE * P], BF16)
        hs = sb("hs", [P, 2, TE, D])
        hd = sb("hd", [P, 2, TE, D])
        hdt = sb("hdt", [P, 2, TE * P])
        agg = sb("agg", [P, 2, TE * P])
        prod = sb("prod", [P, 2, TE * P])
        msg = sb("msg", [P, 2, TE * D])
        ye = sb("ye", [P, BUFS, TE * D])
        oe = sb("oe", [P, BUFS, TE, D])
        bst = sb("bst", [P, TS, 6])
        msum = sb("msum", [P, TS])
        mdif = sb("mdif", [P, TS])
        m2 = sb("m2", [P, TS])
        dsq = sb("dsq", [P, TS])
        mean = sb("mean", [P, 2, TS])
        var = sb("var", [P, 2, TS])
        guard = sb("guard", [P, BUFS, TD + TE])
        sd = sb("sd", [P, 2 * TE])
        rs = sb("rs", [P, 2, 2 * TE])
        scs = sb("scs", [P, 2, TE])
        norms = sb("norms", [P, TE])
        bia = sb("bia", [P, 2, 2 * TE])
        ss = sb("ss", [P, BUFS, TD + TE])
        d2 = sb("d2", [P, TD + TE])
        dd = sb("dd", [P, TD + TE])
        rd = sb("rd", [P, TD + TE])
        junk = sb("junk", [P, TD + TE, D], BF16)
        idx = sb("idx", [P, STEPS, 4, 2, 2], I32)
        idl = sb("idl", [P, Q, 2], I32)
        lohi = sb("lohi", [P, 2, Q, 2])
        nd = sb("nd", [P, Q, 2])
        stage = sb("stage", [P, XBUFS, 3 * TE], I32)
        sstage = sb("sstage", [P, BUFS, TE], I32)
        lstage = sb("lstage", [P, 2, 2], I32)
        nf16 = sb("nf16", [Q, QW], BF16)
        iotaf = sb("iotaf", [P, J], F16)
        rowi = sb("rowi", [Q, 2], I32)
        lim = sb("lim", [Q, 1])
        endc = sb("endc", [Q, 7])
        rows = sb("rows", [1, 9, P])
        flr = sb("flr", [Q, 1])
        fli = sb("fli", [1, 1], I32)
        ucol = sb("ucol", [Q, 1])
        urow = sb("urow", [1, Q])
        umax = sb("umax", [1, 1])
        ufli = sb("ufli", [1, 1], I32)
        lrow = sb("lrow", [P, 2, 2 * D])
        nat = xo[0:Q, 1, 0:5 * QW].bitcast(I32).rearrange("q (a w) -> q a w", a=5)
        natf = xo[0:Q, 0, :].rearrange("q (a w) -> q a w", a=8)
        df, nf, nl, cloc, fsm, flf, onesq, ioq = (ye[0:Q, k // 2, k % 2 * QW:(k % 2 + 1) * QW] for k in range(8))
        iotai = oe[:, 0, :, :].rearrange("p t f -> p (t f)")[:, 0:J].bitcast(I32)
        ohl = ybuf[:, 0, 0:BUFS * LO // 2].bitcast(F16).rearrange("p (b j) -> p b j", b=BUFS)
        ohh = ybuf[:, 1, 0:BUFS * J // 2].bitcast(F16).rearrange("p (b j) -> p b j", b=BUFS)
        ohd = ybuf[:, 2, 0:LO].bitcast(F16)[:, 0:J]
        tabs = hdt[:].rearrange("p b f -> p (b f)")[:, 0:2 * J]
        tabq = agg[:].rearrange("p b f -> p (b f)")[:, 0:2 * J]
        ndq = prod[:, 0, 0:2 * Q]

        masks = xin[:, 0, :].rearrange("p (k w) -> p k w", k=4)
        crow, crowf, cjunk, cio = (xin[:, 1, k * CW:(k + 1) * CW] for k in range(4))
        cioi = xin[:, 2, 0:CW].bitcast(I32)
        crowi = crow.bitcast(I32)
        place = xin[:, 2, CW:CW + 1].bitcast(I32)
        placek = xin[:, 2, CW + 1:CW + 5]
        tie = xin[:, 2, CW + 5:CW + 9]
        guardi = xin[0:1, 2, CW + 9:CW + 10].bitcast(I32)
        thr, dcf, cacc, rank = (xin[:, 2, 3 * P * 2 + k * G:3 * P * 2 + (k + 1) * G] for k in range(4))
        ecol = xin[:, 3, 0:3 * G].bitcast(I32).rearrange("p (g c) -> p g c", c=3)
        estage = xin[:, 3, 3 * G:3 * G + 6].bitcast(I32).rearrange("p (b c) -> p b c", b=2)

        pt = ctx.enter_context(nc.psum_tensor("pt", [P, 2, 512], F32))
        pu = ctx.enter_context(nc.psum_tensor("pu", [P, 2, 512], F32))
        pe_s = ctx.enter_context(nc.psum_tensor("pe_s", [P, 512], F32))
        pe_d = ctx.enter_context(nc.psum_tensor("pe_d", [P, 512], F32))
        pe_m = ctx.enter_context(nc.psum_tensor("pe_m", [P, 512], F32))
        pe_x = ctx.enter_context(nc.psum_tensor("pe_x", [P, 512], F32))
        turned = [pt[:, 0, :], pt[:, 1, :], pu[:, 0, :], pu[:, 1, :], pe_s[:], pe_d[:], pe_m[:], pe_x[:]]

        s_filled = sem("s_filled")
        s_nat = sem("s_nat")
        s_w = sem("s_w")
        s_zero = sem("s_zero")
        s_ident = sem("s_ident")
        s_iota = sem("s_iota")
        s_const = sem("s_const")
        s_ch = sem("s_ch")
        s_endc = sem("s_endc")
        s_carryrow = sem("s_carryrow")
        s_late = sem("s_late")
        s_ends = sem("s_ends")
        s_carry = sem("s_carry")
        s_firstc = sem("s_firstc")
        s_firsts = sem("s_firsts")
        s_totalrow = sem("s_totalrow")
        s_totals = sem("s_totals")
        s_natf = sem("s_natf")
        s_turn = sem("s_turn")
        s_idx = sem("s_idx")
        s_cnt = sem("s_cnt")
        s_ndq = sem("s_ndq")
        s_oh = sem("s_oh")
        s_ohd = sem("s_ohd")
        s_oha = sem("s_oha")
        s_ohu = sem("s_ohu")
        s_tab = sem("s_tab")
        s_tabq = sem("s_tabq")
        s_tabr = sem("s_tabr")
        s_ntab = sem("s_ntab")
        s_nfd = sem("s_nfd")
        s_flag = sem("s_flag")
        s_unsorted = sem("s_unsorted")
        s_udram = sem("s_udram")
        s_urow = sem("s_urow")
        s_uflag = sem("s_uflag")
        u_begin = sem("u_begin")
        u_iota = sem("u_iota")
        u_pad = sem("u_pad")
        u_cols = sem("u_cols")
        u_guard = sem("u_guard")
        u_row = sem("u_row")
        u_used = sem("u_used")
        u_ch = sem("u_ch")
        u_rank = sem("u_rank")
        u_staged = sem("u_staged")
        u_put = sem("u_put")
        u_back = sem("u_back")
        x_loaded = sems("x_loaded")
        x_loaded2 = sems("x_loaded2_")
        same_loaded = sems("same_loaded")
        xs_got = sems("xs_got", XBUFS)
        xd_got = sems("xd_got", XBUFS)
        nsrc_got = sems("nsrc_got", XBUFS)
        out_stored = sems("out_stored")
        late_stored = sems("late_stored")
        scattered = sems("scattered")
        staged = sem("staged")
        sstaged = sem("sstaged")
        bn_done = sem("bn_done")
        st_chain = sem("st_chain")
        mean_ready = sem("mean_ready")
        var_ready = sem("var_ready")
        sd_ready = sem("sd_ready")
        rs_chain = sem("rs_chain")
        affine_ready = sem("affine_ready")
        relu_done = sem("relu_done")
        et_done = sem("et_done")
        hdt_done = sem("hdt_done")
        scan_done = sem("scan_done")
        prod_done = sem("prod_done")
        em_done = sem("em_done")
        msg_done = sem("msg_done")
        ye_done = sem("ye_done")
        t_done = sem("t_done")
        t_evac = sem("t_evac")
        m_done = sem("m_done")
        u_evac = sem("u_evac")
        y_done = sem("y_done")
        ss_done = sem("ss_done")
        d2_ready = sem("d2_ready")
        dd_ready = sem("dd_ready")
        rd_ready = sem("rd_ready")
        f_done = sem("f_done")
        late_got = sems("late_got", 2)
        late_put = sem("late_put")
        lstaged = sem("lstaged")

        def steps(eng, do, last):
            for i in range(UN):
                do(Step(0, i), i)
            with eng.Fori(1, LOOPS) as blk:
                for r in range(UN):
                    do(Step(blk, r), None)
            for i in range(LOOPS * UN, last + 1):
                do(Step(LOOPS, i - LOOPS * UN), i)

        def has(i, d):
            return i is None or 0 <= i + d < STEPS

        def chunk(t, s, i, d):
            if i is not None and i + d == STEPS - 1:
                return t[(STEPS - 1) * CH:N, :].rearrange("(p t) f -> p (t f)", t=TD), LASTP
            return t[bass.ds(s(d) * CH, CH), :].rearrange("(p t) f -> p (t f)", t=TD), P

        block = ctx.enter_context(nc.Block())

        @block.sync
        def _(sp):
            sp.dma_start(w1[:], W1).then_inc(s_w, 16)
            sp.dma_start(w2[:], W2).then_inc(s_w, 16)
            sp.wait_ge(s_filled, 1)
            flat = lambda t, a, b, q: t[a:b].rearrange("(q w) -> q w", q=q)
            sp.dma_start(nat[0:QF, 0, :], flat(dst, 0, QF * QW, QF)).then_inc(s_nat, 16)
            sp.dma_start(nat[QF:Q, 0, 0:QR], flat(dst, QF * QW, E, 1)).then_inc(s_nat, 16)
            sp.dma_start(nat[0:1, 1, 1:QW], flat(dst, 0, QW - 1, 1)).then_inc(s_nat, 16)
            sp.dma_start(nat[1:QF, 1, :], flat(dst, QW - 1, QF * QW - 1, QF - 1)).then_inc(s_nat, 16)
            sp.dma_start(nat[QF:Q, 1, 0:QR + 1], flat(dst, QF * QW - 1, E, 1)).then_inc(s_nat, 16)
            sp.dma_start(nat[0:QF, 2, :], flat(dst, 1, QF * QW + 1, QF)).then_inc(s_nat, 16)
            sp.dma_start(nat[QF:Q, 2, 0:QR - 1], flat(dst, QF * QW + 1, E, 1)).then_inc(s_nat, 16)
            sp.dma_start(nat[0:QF, 3, :], flat(src, 0, QF * QW, QF)).then_inc(s_nat, 16)
            sp.dma_start(nat[QF:Q, 3, 0:QR], flat(src, QF * QW, E, 1)).then_inc(s_nat, 16)
            sp.wait_ge(s_unsorted, 1)
            sp.dma_start(unsortd, ucol[:]).then_inc(s_udram, 16)
            sp.wait_ge(s_udram, 16)
            sp.dma_start(urow[:], unsortd.rearrange("q o -> o q")).then_inc(s_urow, 16)
            sp.wait_ge(s_natf, 1)
            sp.dma_start(nfd, nf16[:]).then_inc(s_nfd, 16)
            sp.wait_ge(s_late, 1)
            sp.dma_start(flagd, fli[:]).then_inc(s_flag, 16)
            sp.wait_ge(s_nfd, 16)
            same_flat = nfd.rearrange("q w -> (q w)")

            def do(s, i):
                if i == BUFS:
                    sp.wait_ge(s_tabr, 1)
                    for h in range(2):
                        sp.dma_start(ntab[h * P * J:(h + 1) * P * J, :].rearrange("(p j) o -> p (j o)", p=P),
                                     tabs[:, h * J:(h + 1) * J]).then_inc(s_ntab, 16)
                if has(i, 0):
                    if has(i, -4):
                        sp.wait_ge(f_done, s(-3))
                    src_rows, np_ = chunk(x, s, i, 0)
                    for half, loaded in enumerate((x_loaded, x_loaded2)):
                        f = slice(half * TD * D // 2, (half + 1) * TD * D // 2)
                        sp.dma_start(xin[0:np_, s.buf(), f], src_rows[:, f]).then_inc(loaded[s.buf()], 16)
                    sp.dma_start(
                        same[:, s.buf(), :],
                        same_flat[bass.ds(s() * (TE * P), TE * P)].rearrange("(o w) -> o w", o=1).to_broadcast([P, TE * P]),
                    ).then_inc(same_loaded[s.buf()], 16)
                if has(i, -4):
                    sp.wait_ge(f_done, s(-3))
                    dst_rows, np_ = chunk(out, s, i, -4)
                    sp.dma_start(dst_rows, xo[0:np_, s.buf(-4, 2), :]).then_inc(out_stored[s.buf(-4)], 16)
                    sp.dma_start(lated[bass.ds(s(-4) * (2 * P), 2 * P), :].rearrange("(h p) w -> p h w", h=2),
                                 oe[:, s.buf(-4), :, :].rearrange("p (h t) f -> p h (t f)", h=2)
                                 ).then_inc(late_stored[s.buf(-4)], 16)

            steps(sp, do, STEPS + 3)
            for b in range(BUFS):
                n = len(range(b, STEPS, BUFS))
                sp.wait_ge(out_stored[b], 16 * n)
                sp.wait_ge(late_stored[b], 16 * n)

        @block.gpsimd
        def _(pool):
            pool.memset(ident[:], 0.0).then_inc(s_zero, 1)
            pool.iota(iotai, pattern=[[1, J]], base=0, channel_multiplier=0)
            pool.iota(rowi[:, 0:1], pattern=[[0, 1]], base=0, channel_multiplier=1).then_inc(s_iota, 1)
            pool.wait_ge(s_zero, 1)
            pool.affine_select(out=ident[:], in_=ident[:], compare_op=ALU.not_equal, fill=1.0, base=0,
                               pattern=[[-1, P]], channel_multiplier=1).then_inc(s_ident, 1)
            pool.wait_ge(s_uflag, 1)
            unsorted = pool.value_load(ufli[:], min_val=0, max_val=1)
            with pool.If(unsorted > 0):
                pool.wait_ge(u_begin, 1)
                for a, row in enumerate((0, 3)):
                    pool.dma_start(padded[a].rearrange("(q w) -> q w", q=Q), nat[:, row, :]).then_inc(u_pad, 16)
                pool.iota(cioi, pattern=[[1, CW]], base=0, channel_multiplier=0)
                pool.iota(place, pattern=[[0, 1]], base=0, channel_multiplier=1)
                pool.memset(guardi, -1).then_inc(u_iota, 1)
                pool.wait_ge(u_pad, 32)
                with nc.allow_non_contiguous_dma(reason="edges to columns, only where dst is out of order"):
                    for a in range(2):
                        for h in range(2):
                            pool.dma_start(ecol[:, h * Q:(h + 1) * Q, 1 + a],
                                           padded[a, h * Q * P:(h + 1) * Q * P].rearrange("(g p) -> p g", p=P)
                                           ).then_inc(u_cols, 16)
                pool.wait_ge(u_iota, 1)
                for at in (0, GP + 1):
                    pool.dma_start(sdst[at:at + 1, :], guardi).then_inc(u_guard, 16)

                def load_chunk(c):
                    pool.dma_start(crowi, padded[0, bass.ds(c * CW, CW)].rearrange("(o w) -> o w", o=1)
                                   .to_broadcast([P, CW])).then_inc(u_row, 16)

                load_chunk(0)
                with pool.Fori(1, GP // CW) as c:
                    pool.wait_ge(u_used, c)
                    load_chunk(c)
                pool.wait_ge(u_rank, 1)
                end_limit = pool.to_reg(GP + 1)

                def stage_group(g, b):
                    pool.tensor_copy(estage[:, b, :], ecol[:, bass.ds(g, 1), :].rearrange("p o c -> p (o c)")
                                     ).then_inc(u_staged, 1)

                def put_group(g, b, first=False, last=False):
                    if not first:
                        pool.wait_ge(u_put, g * 32)
                    pool.wait_ge(u_staged, g + 1)
                    if not last:
                        stage_group(g + 1, 1 - b)
                    for c, to in ((1, sdst), (2, ssrc)):
                        pool.indirect_dma_start(
                            out=to, out_offset=bass.IndirectOffsetOnAxis(ap=estage[:, b, 0:1], axis=0),
                            in_=estage[:, b, c:c + 1], in_offset=None, bounds_check=end_limit, oob_is_err=False,
                        ).then_inc(u_put, 16)

                stage_group(0, 0)
                put_group(0, 0, first=True)
                with pool.Fori(0, G // 2 - 1) as half:
                    put_group(half * 2 + 1, 1)
                    put_group(half * 2 + 2, 0)
                put_group(G - 1, 1, last=True)
                pool.wait_ge(u_put, 32 * G)
                pool.wait_ge(u_guard, 32)
                for row, (rows_of, at) in enumerate(((sdst, 1), (sdst, 0), (sdst, 2), (ssrc, 1))):
                    pool.dma_start(nat[:, row, :], rows_of[at:at + GP, :].rearrange("(q w) o -> q (w o)", q=Q)
                                   ).then_inc(u_back, 16)
            pool.wait_ge(s_idx, 1)
            row_limit = pool.to_reg(N - 1)
            tab_limit = pool.to_reg(LO * J - 1)

            def gather(to, rows, index, limit, done):
                pool.indirect_dma_start(out=to, out_offset=None, in_=rows,
                                        in_offset=bass.IndirectOffsetOnAxis(ap=index, axis=0),
                                        bounds_check=limit, oob_is_err=False).then_inc(done, 16)

            def scatter(rows, index, done):
                pool.indirect_dma_start(out=out, out_offset=bass.IndirectOffsetOnAxis(ap=index, axis=0),
                                        in_=rows, in_offset=None,
                                        bounds_check=row_limit, oob_is_err=False).then_inc(done, 16)

            def stage_gather(s, d):
                pool.tensor_copy(stage[:, s.buf(d, XBUFS), :],
                                 idx[:, bass.ds(s(d), 1), 0:3, :, :].rearrange("p o a q h -> p (o a q h)")
                                 ).then_inc(staged, 1)

            def stage_scatter(s, d):
                pool.tensor_copy(sstage[:, s.buf(d), :],
                                 idx[:, bass.ds(s(d), 1), 3:4, :, :].rearrange("p o a q h -> p (o a q h)")
                                 ).then_inc(sstaged, 1)

            def gather_rows(s, i, d):
                b = s.buf(d, XBUFS)
                if has(i, d - XBUFS):
                    pool.wait_ge(relu_done, s(d - XBUFS + 1))
                    pool.wait_ge(f_done, s(d - XBUFS + 1))
                after = d - XBUFS + 1
                if has(i, after):
                    used = s.buf(after, XBUFS)
                    pool.wait_ge(xs_got[used], s.dma(after, TE, XBUFS))
                    pool.wait_ge(xd_got[used], s.dma(after, TE, XBUFS))
                    pool.wait_ge(nsrc_got[used], s.dma(after, TE, XBUFS))
                pool.wait_ge(staged, s(d + 1))
                if has(i, d + 1):
                    stage_gather(s, d + 1)
                for k in range(TE):
                    gather(xs[:, b, k, :], x, stage[:, b, k:k + 1], row_limit, xs_got[b])
                for k in range(TE):
                    gather(xd[:, b, k, :], x, stage[:, b, TE + k:TE + k + 1], row_limit, xd_got[b])

            def gather_norms(s, d):
                b = s.buf(d, XBUFS)
                for k in range(TE):
                    gather(nsrc[:, b, k:k + 1], ntab, stage[:, b, 2 * TE + k:2 * TE + k + 1], tab_limit, nsrc_got[b])

            stage_gather(Step(0, 0), 0)
            stage_scatter(Step(0, 0), 0)
            for i in range(EARLY):
                gather_rows(Step(0, i), i, 0)
            pool.wait_ge(s_ntab, 32)
            for i in range(NORMS):
                gather_norms(Step(0, i), 0)

            def do(s, i):
                if has(i, NORMS):
                    gather_norms(s, NORMS)
                ahead = AHEAD if i is None or i >= UN else EARLY - sum(j <= i for j in SKIPS)
                if has(i, ahead) and i not in SKIPS:
                    gather_rows(s, i, ahead)
                if has(i, -3):
                    b = s.buf(-3)
                    pool.wait_ge(f_done, s(-2))
                    pool.wait_ge(out_stored[b], s.dma(-3))
                    if has(i, -4):
                        pool.wait_ge(out_stored[s.buf(-4)], s.dma(-4))
                    if has(i, -6):
                        pool.wait_ge(scattered[s.buf(-6)], s.dma(-6, TE))
                    pool.wait_ge(sstaged, s(-2))
                    if has(i, -2):
                        stage_scatter(s, -2)
                    for k in range(TE):
                        scatter(oe[:, b, k, :], sstage[:, b, k:k + 1], scattered[b])

            steps(pool, do, STEPS + 2)
            for b in range(BUFS):
                n = len(range(b, STEPS, BUFS))
                pool.wait_ge(scattered[b], 16 * TE * n)
                pool.wait_ge(out_stored[b], 16 * n)
                pool.wait_ge(late_stored[b], 16 * n)
            pool.wait_ge(s_flag, 16)
            late = pool.value_load(flagd, min_val=0, max_val=1)
            with pool.If(late > 0):
                def bring(q, b):
                    pool.tensor_copy(lstage[:, b, :], idl[:, bass.ds(q, 1), :].rearrange("p o h -> p (o h)")
                                     ).then_inc(lstaged, 1)
                    pool.dma_start(lrow[:, b, :], lated[bass.ds(q * P, P), :]).then_inc(late_got[b], 16)

                def put(q, b, times, first=False, last=False):
                    pool.wait_ge(late_got[b], times * 16 + 16)
                    if not first:
                        pool.wait_ge(late_put, q * 32)
                    pool.wait_ge(lstaged, q + 1)
                    if not last:
                        bring(q + 1, 1 - b)
                    for h in range(2):
                        scatter(lrow[:, b, h * D:(h + 1) * D], lstage[:, b, h:h + 1], late_put)

                bring(0, 0)
                put(0, 0, 0, first=True)
                with pool.Fori(0, Q // 2 - 1) as half:
                    put(half * 2 + 1, 1, half)
                    put(half * 2 + 2, 0, half + 1)
                put(Q - 1, 1, Q // 2 - 1, last=True)
                pool.wait_ge(late_put, 32 * Q)
            pool.nop()

        @block.vector
        def _(dve):
            link = [0]

            def chain(ins):
                link[0] += 1
                ins.then_inc(s_ch, 1)
                dve.wait_ge(s_ch, link[0])

            dve.memset(nat[:, 0, :], int(PAD))
            dve.memset(nat[:, 1:3, :], -1)
            dve.memset(nat[:, 3, :], 0).then_inc(s_filled, 1)
            dve.memset(eps[:], EPS)
            dve.memset(ones[:], 1.0)
            dve.memset(rows[:], 0.0)
            dve.memset(onesq, 1.0)
            dve.memset(guard[:], NORM_MIN * NORM_MIN)
            dve.wait_ge(s_iota, 1)
            dve.tensor_copy(iotaf[:], iotai)
            dve.tensor_scalar(ioq, iotai[0:Q, 0:QW], 1.0, None, ALU.add)
            chain(dve.tensor_scalar(rowi[:, 1:2], rowi[:, 0:1], 1, None, ALU.logical_shift_right))
            dve.tensor_scalar(lim[:], rowi[:, 1:2], float(CH), float(CH - 1), ALU.mult, ALU.add)
            dve.wait_ge(s_ident, 1)
            dve.tensor_scalar(nident[:], ident[:], -1.0, None, ALU.mult).then_inc(s_const, 1)
            dve.wait_ge(s_nat, 16 * 9)
            dve.scalar_tensor_tensor(flf, nat[:, 1, :], 0.0, nat[:, 0, :], ALU.add, ALU.is_gt, accum_out=ucol[:]
                                     ).then_inc(s_unsorted, 1)

            def local(chain):
                chain(dve.tensor_scalar(nat[:, 4, :], nat[:, 0, :], LO - 1, None, ALU.bitwise_and))
                chain(dve.tensor_copy(natf[:, 5, :], nat[:, 4, :]))
                chain(dve.tensor_scalar(nat[:, 4, :], nat[:, 0, :], 8, None, ALU.logical_shift_right))
                chain(dve.tensor_copy(natf[:, 6, :], nat[:, 4, :]))
                chain(dve.tensor_scalar(nat[:, 4, :], nat[:, 3, :], LO - 1, None, ALU.bitwise_and))
                dve.tensor_copy(natf[:, 0, :], nat[:, 3, :])
                chain(dve.tensor_copy(cloc, nat[:, 4, :]))
                chain(dve.tensor_scalar(nat[:, 4, :], nat[:, 3, :], 8, None, ALU.logical_shift_right))
                chain(dve.tensor_copy(fsm, nat[:, 4, :]))
                dve.scalar_tensor_tensor(natf[:, 2, :], cloc, float(J), fsm, ALU.mult, ALU.add)
                chain(dve.tensor_copy(df, nat[:, 0, :]))
                dve.tensor_scalar(natf[:, 1, :], df, float(N - 1), None, ALU.min)
                chain(dve.tensor_tensor(nf, nat[:, 0, :], nat[:, 1, :], ALU.is_equal))
                dve.tensor_tensor(nl, nat[:, 0, :], nat[:, 2, :], ALU.is_equal)
                dve.tensor_copy(nf16[:], nf)
                chain(dve.tensor_tensor_scan(cloc, nf, onesq, 0.0, ALU.mult, ALU.add))
                dve.tensor_copy(endc[:, 0:1], cloc[:, QW - 1:QW])
                dve.tensor_copy(endc[:, 2:3], nf[:, 0:1])
                dve.scalar_tensor_tensor(endc[:, 1:2], cloc[:, QW - 1:QW], float(QW), nf[:, 0:1],
                                         ALU.is_equal, ALU.mult)
                chain(dve.tensor_tensor(fsm, cloc, ioq, ALU.is_equal))
                chain(dve.tensor_scalar(flf, df, lim[:, 0:1], None, ALU.is_gt))
                chain(dve.tensor_tensor(natf[:, 7, :], flf, nl, ALU.max))
                chain(dve.scalar_tensor_tensor(natf[:, 3, :], natf[:, 7, :], PAD, df, ALU.mult, ALU.add))
                chain(dve.tensor_scalar(natf[:, 7, :], flf, -1.0, 1.0, ALU.mult, ALU.add))
                chain(dve.tensor_tensor(flf, natf[:, 7, :], nl, ALU.max))
                chain(dve.scalar_tensor_tensor(natf[:, 4, :], flf, PAD, df, ALU.mult, ALU.add))
                chain(dve.tensor_scalar(flf, natf[:, 4, :], float(N), None, ALU.is_lt))
                chain(dve.tensor_reduce(endc[:, 4:5], flf, AX.X, ALU.max))

            dve.wait_ge(s_unsorted, 1)
            local(chain)
            dve.wait_ge(s_urow, 16)
            chain(dve.tensor_reduce(umax[:], urow[:], AX.X, ALU.max))
            dve.tensor_scalar(ufli[:], umax[:], 1.0, None, ALU.min).then_inc(s_uflag, 1)
            dve.wait_ge(s_uflag, 1)
            unsorted = dve.value_load(ufli[:], min_val=0, max_val=1)
            with dve.If(unsorted > 0):
                ulink = [0]

                def uchain(ins, after=0):
                    ulink[0] += 1
                    ins.then_inc(u_ch, 1)
                    dve.wait_ge(u_ch, ulink[0] + after)

                dve.nop().then_inc(u_begin, 1)
                dve.wait_ge(u_iota, 1)
                dve.wait_ge(u_cols, 64)
                dve.tensor_copy(cio, cioi)
                for k in range(4):
                    last = dve.tensor_scalar(placek[:, k:k + 1], place, float(k * P), None, ALU.add)
                uchain(last)
                for k in range(4):
                    dve.tensor_scalar(masks[:, k, :], cio, placek[:, k:k + 1], None, ALU.is_lt)
                dve.memset(rank, 0.0)
                uchain(dve.tensor_copy(dcf, ecol[:, :, 1]))
                uchain(dve.tensor_scalar(thr, dcf, 0.5, None, ALU.add))
                before = ulink[0]
                each = 1 + G + 4 + 2
                with dve.Fori(0, GP // CW) as c:
                    dve.wait_ge(u_row, c * 16 + 16)
                    dve.wait_ge(u_ch, c * each + before)
                    dve.tensor_copy(crowf, crowi).then_inc(u_used, 1)
                    dve.wait_ge(u_used, c + 1)
                    dve.tensor_copy(thr[:, bass.ds(c * 4, 4)], dcf[:, bass.ds(c * 4, 4)]).then_inc(u_ch, 1)
                    with dve.Fori(0, G) as g:
                        dve.wait_ge(u_ch, c * each + g + (before + 1))
                        dve.tensor_scalar(cjunk, crowf, thr[:, bass.ds(g, 1)], None, ALU.is_lt, ALU.add,
                                          accum_out=cacc[:, bass.ds(g, 1)]).then_inc(u_ch, 1)
                    for k in range(4):
                        dve.wait_ge(u_ch, c * each + (before + 1 + G + k))
                        dve.scalar_tensor_tensor(cjunk, crowf, dcf[:, bass.ds(c * 4 + k, 1)], masks[:, k, :],
                                                 ALU.is_equal, ALU.mult, accum_out=tie[:, k:k + 1]).then_inc(u_ch, 1)
                    dve.wait_ge(u_ch, c * each + (before + 1 + G + 4))
                    dve.tensor_tensor(rank, rank, cacc, ALU.add).then_inc(u_ch, 1)
                    dve.wait_ge(u_ch, c * each + (before + 2 + G + 4))
                    dve.tensor_tensor(rank[:, bass.ds(c * 4, 4)], rank[:, bass.ds(c * 4, 4)], tie, ALU.add
                                      ).then_inc(u_ch, 1)
                dve.wait_ge(u_ch, GP // CW * each + before)
                dve.tensor_scalar(ecol[:, :, 0], rank, 1.0, None, ALU.add).then_inc(u_rank, 1)
                dve.wait_ge(u_rank, 1)
                dve.wait_ge(u_back, 64)
                local(lambda ins: uchain(ins, GP // CW * each))
            dve.tensor_copy(endc[:, 3:4], endc[:, 0:1]).then_inc(s_endc, 1)
            dve.wait_ge(s_ends, 1)
            for k in range(3):
                dve.tensor_copy(rows[0:1, k, 0:Q], pe_s[0:1, k * P:k * P + Q])
            chain(dve.tensor_reduce(rows[0:1, 5, 0:1], pe_s[0:1, 3 * P:3 * P + Q], AX.X, ALU.max))
            dve.tensor_copy(fli[:], rows[0:1, 5, 0:1]).then_inc(s_late, 1)
            chain(dve.tensor_tensor_scan(rows[0:1, 3, 0:Q], rows[0:1, 1, 0:Q], rows[0:1, 0, 0:Q], 0.0,
                                         ALU.mult, ALU.add))
            dve.tensor_tensor(rows[0:1, 4, 1:Q], rows[0:1, 2, 1:Q], rows[0:1, 3, 0:Q - 1], ALU.mult).then_inc(s_carryrow, 1)
            dve.wait_ge(s_carry, 1)
            chain(dve.tensor_copy(flr[:], pe_d[0:Q, 0:1]))
            chain(dve.scalar_tensor_tensor(natf[:, 7, :], fsm, flr[:, 0:1], cloc, ALU.mult, ALU.add))
            chain(dve.tensor_scalar(fsm, nl, -1.0, 1.0, ALU.mult, ALU.add))
            chain(dve.tensor_tensor(flf, fsm, natf[:, 7, :], ALU.mult))
            chain(dve.tensor_tensor_scan(cloc[:, ::-1], nl[:, ::-1], flf[:, ::-1], 0.0, ALU.mult, ALU.add))
            dve.tensor_copy(endc[:, 5:6], cloc[:, 0:1])
            dve.tensor_scalar(endc[:, 6:7], cloc[:, 0:1], 0.0, None, ALU.is_equal).then_inc(s_firstc, 1)
            chain(dve.tensor_scalar(fsm, cloc, 0.0, None, ALU.is_equal))
            dve.wait_ge(s_firsts, 1)
            for k in range(2):
                last = dve.tensor_copy(rows[0:1, 6 + k, 0:Q], pe_s[0:1, k * P:k * P + Q])
            chain(last)
            dve.tensor_tensor_scan(rows[0:1, 8, Q - 1::-1], rows[0:1, 7, Q - 1::-1], rows[0:1, 6, Q - 1::-1], 0.0,
                                   ALU.mult, ALU.add).then_inc(s_totalrow, 1)
            dve.wait_ge(s_totals, 1)
            chain(dve.tensor_copy(flr[:], pe_d[0:Q, 0:1]))
            dve.scalar_tensor_tensor(natf[:, 7, :], fsm, flr[:, 0:1], cloc, ALU.mult, ALU.add
                                     ).then_inc(s_natf, 1)
            dve.wait_ge(s_turn, 1)
            for h in range(2):
                for a in range(8):
                    col = turned[a][:, h * P:h * P + Q]
                    if a < 4:
                        dve.tensor_copy(idx[:, :, a, :, h], col.rearrange("p (b q) -> p b q", q=2))
                    elif a == 4:
                        dve.tensor_copy(idl[:, :, h], col)
                    elif a < 7:
                        dve.tensor_copy(lohi[:, a - 5, :, h], col)
                    else:
                        last = dve.tensor_copy(nd[:, :, h], col)
            last.then_inc(s_idx, 1)
            dve.wait_ge(s_idx, 1)
            dve.wait_ge(s_ndq, 1)
            dve.reciprocal(nd[:].rearrange("p q h -> p (q h)"), ndq)
            col = lohi[:].rearrange("p a q h -> p a (q h)")

            def onehot(g, k, wait):
                if wait:
                    dve.wait_ge(s_ohu, g - (BUFS - 1))
                last = dve.tensor_scalar(ohl[:, k, :], iotaf[:, 0:LO], col[:, 0, bass.ds(g, 1)], None, ALU.is_equal)
                if k < BUFS - 1:
                    last = dve.tensor_scalar(ohh[:, k, :], iotaf[:], col[:, 1, bass.ds(g, 1)], None, ALU.is_equal)
                last.then_inc(s_oh, 1)

            for k in range(BUFS):
                onehot(k, k, False)
            with dve.Fori(0, TURNS) as b:
                for k in range(HU):
                    onehot(b * HU + (BUFS + k), k % BUFS, True)
            dve.wait_ge(s_ohu, G)
            dve.tensor_scalar(tabs[:, 0:J], pt[:, 0, 0:J], 1.0, None, ALU.max)
            dve.tensor_scalar(tabs[:, J:2 * J], pt[:, 1, 0:J], 1.0, None, ALU.max).then_inc(s_tab, 1)
            dve.wait_ge(s_tabq, 1)
            dve.reciprocal(tabs, tabq).then_inc(s_tabr, 1)

            ndf = nd[:].rearrange("p q h -> p (q h)")

            def stats_rows(s, d):
                b, e = s.buf(d), s.buf(d, XBUFS)
                dve.wait_ge(x_loaded[b], s.dma(d))
                for t in range(TD):
                    if t == TD // 2:
                        dve.wait_ge(x_loaded2[b], s.dma(d))
                    dve.bn_stats(bst[:, t, :], xin[:, b, t * D:(t + 1) * D])
                dve.wait_ge(xs_got[e], s.dma(d, TE, XBUFS))
                for t in range(TE):
                    dve.bn_stats(bst[:, TD + t, :], xs[:, e, t, :])
                dve.wait_ge(xd_got[e], s.dma(d, TE, XBUFS))
                for t in range(TE):
                    last = dve.bn_stats(bst[:, TD + TE + t, :], xd[:, e, t, :])
                last.then_inc(bn_done, 1)

            def stats_sums(s, d):
                dve.wait_ge(bn_done, s(d + 1))
                dve.tensor_tensor(msum[:], bst[:, :, 1], bst[:, :, 4], ALU.add)
                dve.tensor_tensor(mdif[:], bst[:, :, 1], bst[:, :, 4], ALU.subtract)
                dve.tensor_tensor(m2[:], bst[:, :, 2], bst[:, :, 5], ALU.add).then_inc(st_chain, 1)

            def stats_mean(s, d):
                dve.wait_ge(st_chain, s(d) * 2 + 1)
                dve.tensor_scalar(mean[:, s.buf(d, 2), :], msum[:], 0.5, None, ALU.mult).then_inc(mean_ready, 1)
                dve.scalar_tensor_tensor(dsq[:], mdif[:], 0.25, mdif[:], ALU.mult, ALU.mult).then_inc(st_chain, 1)

            def stats_var(s, d):
                dve.wait_ge(st_chain, s(d) * 2 + 2)
                dve.scalar_tensor_tensor(var[:, s.buf(d, 2), :], m2[:], 1.0 / D, dsq[:], ALU.mult, ALU.add
                                         ).then_inc(var_ready, 1)

            def stats_guard(s, d):
                dve.wait_ge(var_ready, s(d + 1))
                dve.tensor_scalar(guard[:, s.buf(d), 0:TD], var[:, s.buf(d, 2), 0:TD], EPS, NORM_MIN * NORM_MIN,
                                  ALU.add, ALU.mult)

            def out_edges(s, first, last):
                b, e = s.buf(-2), s.buf(-2, XBUFS)
                for t in range(first, last):
                    dve.scalar_tensor_tensor(oe[:, b, t, :], ye[:, b, t * D:(t + 1) * D], rd[:, TD + t:TD + t + 1],
                                             xd[:, e, t, :], ALU.mult, ALU.add)

            def out_dense(s):
                b = s.buf(-2)
                for t in range(TD):
                    f = slice(t * D, (t + 1) * D)
                    last = dve.scalar_tensor_tensor(xo[:, s.buf(-2, 2), f], ybuf[:, b, f], rd[:, t:t + 1],
                                                    xin[:, b, f], ALU.mult, ALU.add)
                return last

            for piece in (stats_rows, stats_sums, stats_mean, stats_var, stats_guard):
                piece(Step(0, 0), 0)

            def do(s, i):
                if has(i, -1):
                    b, h, hp = s.buf(-1), s.buf(-1, 2), s.buf(-2, 2)
                    dve.wait_ge(et_done, s())
                    dve.wait_ge(same_loaded[b], s.dma(-1))
                    if has(i, -3):
                        dve.wait_ge(em_done, s(-2))
                    if i == 1:
                        start = 0.0
                        dve.wait_ge(s_tabr, 1)
                    else:
                        dve.wait_ge(scan_done, s(-1))
                        start = agg[:, hp, TE * P - 1:TE * P]
                    dve.tensor_tensor_scan(agg[:, h, :], same[:, b, :], pe_s[:], start, ALU.mult, ALU.add
                                           ).then_inc(scan_done, 1)
                if has(i, 0):
                    e, h = s.buf(0, XBUFS), s.buf(0, 2)
                    dve.wait_ge(sd_ready, s(1))
                    if has(i, -2):
                        dve.wait_ge(relu_done, s(-1))
                    dve.reciprocal(rs[:, h, :], sd[:]).then_inc(rs_chain, 1)
                    dve.wait_ge(nsrc_got[e], s.dma(0, TE, XBUFS))
                    dve.tensor_tensor(norms[:], nsrc[:, e, :], ndf[:, bass.ds(s() * TE, TE)], ALU.mult
                                      ).then_inc(rs_chain, 1)
                if has(i, -1):
                    hh = s.buf(-1, 2)
                    dve.wait_ge(scan_done, s())
                    dve.wait_ge(hdt_done, s())
                    dve.tensor_tensor(prod[:, hh, :], agg[:, hh, :], hdt[:, hh, :], ALU.mult).then_inc(prod_done, 1)
                if has(i, 0):
                    dve.wait_ge(rs_chain, s() * 3 + 2)
                    dve.tensor_tensor(scs[:, h, :], rs[:, h, 0:TE], norms[:], ALU.mult).then_inc(rs_chain, 1)
                    dve.scalar_tensor_tensor(bia[:, h, TE:2 * TE], mean[:, h, TD + TE:TS], -1.0, rs[:, h, TE:2 * TE],
                                             ALU.mult, ALU.mult)
                if has(i, -2):
                    dve.wait_ge(ss_done, s(-1))
                    dve.tensor_tensor(d2[:], ss[:, s.buf(-2), :], guard[:, s.buf(-2), :], ALU.max).then_inc(d2_ready, 1)
                if has(i, 0):
                    dve.wait_ge(rs_chain, s() * 3 + 3)
                    dve.scalar_tensor_tensor(bia[:, h, 0:TE], mean[:, h, TD:TD + TE], -1.0, scs[:, h, :],
                                             ALU.mult, ALU.mult).then_inc(affine_ready, 1)
                if has(i, -1):
                    yb = ybuf[:, s.buf(-1), :]
                    dve.wait_ge(u_evac, s() * NQ)
                    dve.scalar_tensor_tensor(yb, yb, SLOPE, yb, ALU.mult, ALU.max).then_inc(y_done, 1)
                if has(i, 1):
                    stats_rows(s, 1)
                if has(i, -2):
                    dve.wait_ge(dd_ready, s(-1))
                    dve.reciprocal(rd[:], dd[:]).then_inc(rd_ready, 1)
                if has(i, 1):
                    stats_sums(s, 1)
                if has(i, -2):
                    dve.wait_ge(rd_ready, s(-1))
                    if has(i, -6):
                        dve.wait_ge(scattered[s.buf(-2)], s.dma(-6, TE))
                        dve.wait_ge(late_stored[s.buf(-2)], s.dma(-6))
                    out_edges(s, 0, TE // 2)
                if has(i, 1):
                    stats_mean(s, 1)
                if has(i, -2):
                    out_edges(s, TE // 2, TE)
                if has(i, 1):
                    stats_var(s, 1)
                if has(i, -2):
                    if has(i, -4):
                        dve.wait_ge(out_stored[s.buf(-4)], s.dma(-4))
                    out_dense(s).then_inc(f_done, 1)
                if has(i, 1):
                    stats_guard(s, 1)
                if has(i, -1):
                    mb = msg[:, s.buf(-1, 2), :]
                    dve.wait_ge(msg_done, s())
                    dve.scalar_tensor_tensor(ye[:, s.buf(-1), :], mb, SLOPE, mb, ALU.mult, ALU.max
                                             ).then_inc(ye_done, 1)

            steps(dve, do, STEPS + 1)

        @block.scalar
        def _(act):
            act.wait_ge(s_idx, 1)
            act.activation(ndq, nd[:].rearrange("p q h -> p (q h)"), ACT.Sqrt).then_inc(s_ndq, 1)

            def onehot(g, turn, first=False):
                if not first:
                    act.wait_ge(s_oha, turn)
                act.activation(ohd, iotaf[:], ACT.Abs, scale=-1.0,
                               bias=lohi[:].rearrange("p a q h -> p a (q h)")[:, 1, bass.ds(g, 1)]).then_inc(s_ohd, 1)
                act.wait_ge(s_ohd, turn + 1)
                if not first:
                    act.wait_ge(s_ohu, g - (BUFS - 1))
                act.activation(ohh[:, BUFS - 1, :], ohd, ACT.Relu, scale=-1.0, bias=1.0).then_inc(s_oha, 1)

            onehot(BUFS - 1, 0, first=True)
            with act.Fori(0, TURNS) as b:
                for k in range(HU // BUFS):
                    onehot(b * HU + (2 * BUFS - 1 + k * BUFS), b * (HU // BUFS) + (k + 1))
            act.wait_ge(s_tab, 1)
            act.activation(tabq, tabs, ACT.Sqrt).then_inc(s_tabq, 1)

            def do(s, i):
                def relu_quarter(q):
                    act.wait_ge(t_done, s() * NQ + (q + 1))
                    if q >= 2 or has(i, -1):
                        act.wait_ge(m_done, s() * NQ + (q - 1))
                    act.activation(ct[:, q % 2, :], pt[:, q % 2, :], ACT.Relu).then_inc(t_evac, 1)

                def copy_quarter(q):
                    act.wait_ge(m_done, s() * NQ + (q + 1))
                    act.copy(ybuf[:, s.buf(), q * 512:(q + 1) * 512], pu[:, q % 2, :]).then_inc(u_evac, 1)

                def relu_rows(to, rows, scale, bias):
                    for t in range(TE):
                        last = act.activation(to[:, t, :], rows[:, t, :], ACT.Relu, bias=bias[:, t:t + 1],
                                              scale=scale[:, t:t + 1])
                    return last

                def squares(first, last):
                    b = s.buf(-1)
                    for t in range(first, last):
                        act.activation(junk[:, t, :], ybuf[:, b, t * D:(t + 1) * D], ACT.Square,
                                       accum_out=ss[:, b, t:t + 1])

                if has(i, 0):
                    act.wait_ge(var_ready, s(1))
                    if has(i, -1):
                        act.wait_ge(affine_ready, s())
                    act.activation(sd[:], var[:, s.buf(0, 2), TD:TS], ACT.Sqrt, bias=eps[:, 0:1]).then_inc(sd_ready, 1)
                if has(i, -1):
                    act.wait_ge(et_done, s())
                    if has(i, -3):
                        act.wait_ge(em_done, s(-2))
                        act.wait_ge(prod_done, s(-2))
                    if i in (1, 2):
                        act.wait_ge(s_ntab, 32)
                    act.copy(hdt[:, s.buf(-1, 2), :], pe_d[:]).then_inc(hdt_done, 1)
                if has(i, 0):
                    relu_quarter(0)
                    relu_quarter(1)
                    if has(i, -4):
                        act.wait_ge(f_done, s(-3))
                    copy_quarter(0)
                if has(i, -2):
                    b = s.buf(-2)
                    act.wait_ge(ye_done, s(-1))
                    for t in range(TE):
                        last = act.activation(junk[:, TD + t, :], ye[:, b, t * D:(t + 1) * D], ACT.Square,
                                              accum_out=ss[:, b, TD + t:TD + t + 1])
                    last.then_inc(ss_done, 1)
                if has(i, 0):
                    e, h = s.buf(0, XBUFS), s.buf(0, 2)
                    act.wait_ge(affine_ready, s(1))
                    if has(i, -2):
                        act.wait_ge(et_done, s(-1))
                    relu_rows(hs[:, h], xs[:, e], scs[:, h], bia[:, h, 0:TE])
                    relu_quarter(2)
                    copy_quarter(1)
                if has(i, -2):
                    act.wait_ge(d2_ready, s(-1))
                    if has(i, -3):
                        act.wait_ge(rd_ready, s(-2))
                    act.activation(dd[:], d2[:], ACT.Sqrt).then_inc(dd_ready, 1)
                if has(i, 0):
                    relu_rows(hd[:, h], xd[:, e], rs[:, h, TE:2 * TE], bia[:, h, TE:2 * TE]).then_inc(relu_done, 1)
                    relu_quarter(3)
                    copy_quarter(2)
                if has(i, -1):
                    act.wait_ge(y_done, s())
                    squares(0, 4)
                    act.wait_ge(em_done, s())
                    if has(i, -3):
                        act.wait_ge(ye_done, s(-2))
                    act.copy(msg[:, s.buf(-1, 2), :], pe_m[:]).then_inc(msg_done, 1)
                if has(i, 0):
                    copy_quarter(3)
                if has(i, -1):
                    squares(4, TD)

            steps(act, do, STEPS + 1)

        @block.tensor
        def _(pe):
            pe.wait_ge(s_const, 1)
            pe.wait_ge(s_endc, 1)
            for k, c in enumerate((0, 1, 2, 4)):
                last = pe.matmul(pe_s[0:1, k * P:k * P + Q], endc[:, c:c + 1], ident[0:Q, 0:Q], start=True, stop=True)
            last.then_inc(s_ends, 1)
            pe.wait_ge(s_carryrow, 1)
            pe.matmul(pe_d[0:Q, 0:1], rows[0:1, 4, 0:Q], ones[0:1, 0:1], start=True, stop=True).then_inc(s_carry, 1)
            pe.wait_ge(s_firstc, 1)
            for k in range(2):
                last = pe.matmul(pe_s[0:1, k * P:k * P + Q], endc[:, 5 + k:6 + k], ident[0:Q, 0:Q], start=True, stop=True)
            last.then_inc(s_firsts, 1)
            pe.wait_ge(s_totalrow, 1)
            pe.matmul(pe_d[0:Q, 0:1], rows[0:1, 8, 1:Q + 1], ones[0:1, 0:1], start=True, stop=True).then_inc(s_totals, 1)
            pe.wait_ge(s_natf, 1)
            for a in range(8):
                for h in range(2):
                    last = pe.transpose(turned[a][:, h * P:h * P + Q], natf[:, a, h * P:(h + 1) * P], ident[0:Q, 0:Q])
            last.then_inc(s_turn, 1)
            pe.wait_ge(s_idx, 1)

            def count(g, k, first, final, turn):
                pe.wait_ge(s_oh, g + 1)
                if k == BUFS - 1:
                    pe.wait_ge(s_oha, turn + 1)
                for h in range(2):
                    last = pe.matmul(pt[:, h, 0:J], ohl[:, k, h * P:(h + 1) * P], ohh[:, k, :], start=first, stop=final)
                last.then_inc(s_ohu, 1)

            def count_turn(b, final=False):
                for k in range(HU):
                    count(b * HU + (BUFS + k), k % BUFS, False, final and k == HU - 1, b * (HU // BUFS) + (1 + k // BUFS))

            for k in range(BUFS):
                count(k, k, k == 0, False, 0)
            with pe.Fori(0, TURNS - 1) as b:
                count_turn(b)
            count_turn(TURNS - 1, final=True)
            pe.wait_ge(s_tab, 1)
            pe.wait_ge(s_w, 32)

            def do(s, i):
                def turn_quarter(q):
                    if q >= 2 or has(i, -1):
                        pe.wait_ge(t_evac, s() * NQ + (q - 1))
                    for t in range(4):
                        f = slice(t * D, (t + 1) * D)
                        col = q * 4 + t
                        pe.matmul(pt[:, q % 2, f], xin[:, s.buf(), col * D:(col + 1) * D], ident[:],
                                  is_transpose=True, start=True, stop=False)
                        last = pe.matmul(pt[:, q % 2, f], mean[:, s.buf(0, 2), col:col + 1].to_broadcast([P, D]),
                                         nident[:], start=False, stop=True)
                    last.then_inc(t_done, 1)

                def mul_quarter(q):
                    pe.wait_ge(t_evac, s() * NQ + (q + 1))
                    if q >= 2 or has(i, -1):
                        pe.wait_ge(u_evac, s() * NQ + (q - 1))
                    for t in range(4):
                        f = slice(t * D, (t + 1) * D)
                        last = pe.matmul(pu[:, q % 2, f], ct[:, q % 2, f], w1[:], start=True, stop=True)
                    last.then_inc(m_done, 1)

                if has(i, 0):
                    pe.wait_ge(mean_ready, s(1))
                    turn_quarter(0)
                    turn_quarter(1)
                    mul_quarter(0)
                    turn_quarter(2)
                    mul_quarter(1)
                    turn_quarter(3)
                if has(i, -1):
                    h = s.buf(-1, 2)
                    pe.wait_ge(hdt_done, s())
                    pe.wait_ge(prod_done, s())
                    if has(i, -2):
                        pe.wait_ge(msg_done, s(-1))
                    for t in range(TE):
                        f = slice(t * D, (t + 1) * D)
                        pe.matmul(pe_m[:, f], hdt[:, h, f], w1[:], start=True, stop=False)
                        pe.matmul(pe_m[:, f], agg[:, h, f], w1[:], start=False, stop=False)
                        last = pe.matmul(pe_m[:, f], prod[:, h, f], w2[:], start=False, stop=True)
                    last.then_inc(em_done, 1)
                if has(i, 0):
                    mul_quarter(2)
                    mul_quarter(3)
                    h = s.buf(0, 2)
                    pe.wait_ge(relu_done, s(1))
                    if has(i, -1):
                        pe.wait_ge(scan_done, s())
                        pe.wait_ge(hdt_done, s())
                    for t in range(TE):
                        f = slice(t * D, (t + 1) * D)
                        pe.transpose(pe_s[:, f], hs[:, h, t, :], ident[:])
                        last = pe.transpose(pe_d[:, f], hd[:, h, t, :], ident[:])
                    last.then_inc(et_done, 1)

            steps(pe, do, STEPS)


def kernel(**inputs):
    import concourse.bacc as bacc
    from concourse.bass_utils import run_bass_kernel_spmd

    nc = bacc.Bacc("TRN2", target_bir_lowering=False, num_devices=1)
    arrays, args = {}, []
    for name in ("x", "src", "dst", "L0_gnn_W1", "L0_gnn_W2"):
        a = np.ascontiguousarray(inputs[name])
        arrays[f"in_{name}"] = a
        args.append(nc.dram_tensor(f"in_{name}", a.shape, mybir.dt.from_np(a.dtype), kind="ExternalInput").ap())
    out = nc.dram_tensor("out", arrays["in_x"].shape, F32, kind="ExternalOutput").ap()
    gnn_preln_kernel(nc, *args, out)
    r = run_bass_kernel_spmd(nc, [arrays], core_ids=[0])
    return r.results[0]["out"]
```
